# Optimizing a Trainium2 kernel written in Bass

```python
import numpy as np
import jax
import jax.numpy as jnp

def _softmax(x, axis=-1):
    return jax.nn.softmax(x, axis=axis)

def _gelu(x):
    return jax.nn.gelu(x, approximate=True)

def _silu(x):
    return jax.nn.silu(x)

def _sigmoid(x):
    return jax.nn.sigmoid(x)

def _layernorm(x, axis=-1, eps=1e-05):
    m = jnp.mean(x, axis=axis, keepdims=True)
    v = jnp.var(x, axis=axis, keepdims=True)
    return (x - m) / jnp.sqrt(v + eps)

def _scatter_add(tgt, idx, src, axis=0):
    return tgt.at[idx].add(src)

def _segment_sum(src, seg, n):
    return jax.ops.segment_sum(src, seg, n)
kernel_name = 'mk_adj_resnorm_d2_adj_r2_9e1e99'

def setup_inputs(seed: int=0):
    np.random.seed(seed)
    _w = jnp.asarray

    def _rec_inputs():
        import jax
        import jax.numpy as jnp
        _gk = jax.random.key(seed)
        x = -0.0002928 + 1 * jax.random.normal(jax.random.fold_in(_gk, 1), (64, 128, 256), jnp.float32)
        _a = jax.random.bernoulli(jax.random.fold_in(_gk, 2), 0.0625, (64, 128, 128))
        _a = jnp.logical_or(_a, jnp.swapaxes(_a, -1, -2))
        _a = jnp.logical_or(_a, jnp.eye(128, dtype=bool))
        _af = _a.astype(jnp.float32)
        _af = _af * jax.random.uniform(jax.random.fold_in(_gk, 3), (64, 128, 128), jnp.float32, 0.05, 1)
        adj = _af
        return (x, adj)
    x, adj = _rec_inputs()

    def _L0_gnn_setup():
        import jax, jax.numpy as jnp
        import numpy as np
        B, N, DIN, DOUT, K = (4, 1024, 256, 256, 3)
        key = jax.random.key(seed)
        ks = jax.random.split(key, 8)
        X = jax.random.normal(ks[0], (B, N, DIN), dtype=jnp.float32)
        A = jax.random.uniform(ks[1], (B, N, N), dtype=jnp.float32)
        Wv = jax.random.normal(ks[2], (DIN, DOUT), dtype=jnp.float32) * 0.02
        bv = jax.random.normal(ks[3], (DOUT,), dtype=jnp.float32) * 0.02
        aw = jax.random.normal(ks[4], (2 * DOUT, 1), dtype=jnp.float32) * 0.05
        ab = jax.random.normal(ks[5], (1,), dtype=jnp.float32) * 0.05
        Wk = jax.random.normal(ks[6], (K, DIN, DOUT), dtype=jnp.float32) * 0.02
        bk = jax.random.normal(ks[7], (K, DOUT), dtype=jnp.float32) * 0.02
        return {'X': X, 'A': A, 'Wv': Wv, 'bv': bv, 'aw': aw, 'ab': ab, 'Wk': Wk, 'bk': bk}
    _L0_gnn_all = _L0_gnn_setup()
    _L0_gnn_in = {k: v for k, v in _L0_gnn_all.items() if k in ('Wv', 'bv', 'aw', 'ab', 'Wk', 'bk')}
    del _L0_gnn_all

    def _L1_gnn_setup():
        import jax, jax.numpy as jnp
        import numpy as np
        B, N, D = (8, 1024, 256)
        key = jax.random.key(seed)
        ks = jax.random.split(key, 8)
        scale = 0.5 / np.sqrt(D)
        x = jax.random.normal(ks[0], (B, N, D), dtype=jnp.float32)
        adj = jax.random.uniform(ks[1], (B, N, N), dtype=jnp.float32)
        Wq_w = jax.random.normal(ks[2], (D, D), dtype=jnp.float32) * scale
        Wk_w = jax.random.normal(ks[3], (D, D), dtype=jnp.float32) * scale
        Wv_w = jax.random.normal(ks[4], (D, D), dtype=jnp.float32) * scale
        Wq_b = jnp.zeros((D,), dtype=jnp.float32)
        Wk_b = jnp.zeros((D,), dtype=jnp.float32)
        Wv_b = jnp.zeros((D,), dtype=jnp.float32)
        return {'x': x, 'adj': adj, 'Wq_w': Wq_w, 'Wq_b': Wq_b, 'Wk_w': Wk_w, 'Wk_b': Wk_b, 'Wv_w': Wv_w, 'Wv_b': Wv_b}
    _L1_gnn_all = _L1_gnn_setup()
    _L1_gnn_in = {k: v for k, v in _L1_gnn_all.items() if k in ('Wq_w', 'Wq_b', 'Wk_w', 'Wk_b', 'Wv_w', 'Wv_b')}
    del _L1_gnn_all
    return {'x': x, 'adj': adj, 'L0_gnn_Wv': _L0_gnn_in['Wv'], 'L0_gnn_bv': _L0_gnn_in['bv'], 'L0_gnn_aw': _L0_gnn_in['aw'], 'L0_gnn_ab': _L0_gnn_in['ab'], 'L0_gnn_Wk': _L0_gnn_in['Wk'], 'L0_gnn_bk': _L0_gnn_in['bk'], 'L1_gnn_Wq_w': _L1_gnn_in['Wq_w'], 'L1_gnn_Wq_b': _L1_gnn_in['Wq_b'], 'L1_gnn_Wk_w': _L1_gnn_in['Wk_w'], 'L1_gnn_Wk_b': _L1_gnn_in['Wk_b'], 'L1_gnn_Wv_w': _L1_gnn_in['Wv_w'], 'L1_gnn_Wv_b': _L1_gnn_in['Wv_b']}

def reference(x, adj, L0_gnn_Wv, L0_gnn_bv, L0_gnn_aw, L0_gnn_ab, L0_gnn_Wk, L0_gnn_bk, L1_gnn_Wq_w, L1_gnn_Wq_b, L1_gnn_Wk_w, L1_gnn_Wk_b, L1_gnn_Wv_w, L1_gnn_Wv_b):
    import jax
    import jax.numpy as jnp

    def _L0_gnn_ref(X, A, Wv, bv, aw, ab, Wk, bk):
        import jax, jax.numpy as jnp
        import numpy as np
        B, N, DIN, DOUT, K = (4, 1024, 256, 256, 3)
        d = Wv.shape[1]
        Xw = X @ Wv + bv
        sj = Xw @ aw[:d, 0]
        si = Xw @ aw[d:, 0]
        e = jax.nn.leaky_relu(sj[:, None, :] + si[:, :, None] + ab[0], negative_slope=0.2)
        alpha_matrix = A * jnp.exp(e)
        transition = alpha_matrix / (jnp.sum(alpha_matrix, axis=-1, keepdims=True) + 1e-12)
        H = jnp.zeros(X.shape[:-1] + (d,), dtype=X.dtype)
        Xk = X
        for k in range(Wk.shape[0]):
            H = H + Xk @ Wk[k] + bk[k]
            Xk = jnp.einsum('bij,bjd->bid', transition, Xk)
        return jax.nn.relu(H)

    def _L1_gnn_ref(x, adj, Wq_w, Wq_b, Wk_w, Wk_b, Wv_w, Wv_b):
        import jax, jax.numpy as jnp
        import numpy as np
        B, N, D = (8, 1024, 256)
        query = jnp.einsum('bnd,od->bno', x, Wq_w) + Wq_b
        keyt = jnp.einsum('bnd,od->bno', x, Wk_w) + Wk_b
        value = jnp.einsum('bnd,od->bno', x, Wv_w) + Wv_b
        weight = jnp.einsum('bqd,bkd->bqk', query, keyt)
        weight = adj * jnp.exp(weight)
        weight = weight / jnp.sum(weight, axis=2, keepdims=True)
        return jnp.einsum('bqk,bkd->bqd', weight, value)
    x = _layernorm(x + _L0_gnn_ref(x, adj, L0_gnn_Wv, L0_gnn_bv, L0_gnn_aw, L0_gnn_ab, L0_gnn_Wk, L0_gnn_bk), axis=-1)
    x = _layernorm(x + _L1_gnn_ref(x, adj, L1_gnn_Wq_w, L1_gnn_Wq_b, L1_gnn_Wk_w, L1_gnn_Wk_b, L1_gnn_Wv_w, L1_gnn_Wv_b), axis=-1)
    return x

_drawn_inputs = setup_inputs


def setup_inputs(seed=0):
    import zlib

    import numpy as np

    out = dict(_drawn_inputs(seed))
    spreads = {'L1_gnn_Wq_b': (0.0, 0.1), 'L1_gnn_Wk_b': (0.0, 0.8), 'L1_gnn_Wv_b': (0.0, 0.1)}
    factors = {'L0_gnn_Wv': 3.628, 'L0_gnn_bv': 8.0, 'L0_gnn_aw': 3.695}
    for name, (base, spread) in spreads.items():
        noise = np.random.default_rng([zlib.crc32(name.encode()), seed]).standard_normal(out[name].shape)
        drawn = base * np.exp(spread * noise) if base else spread * noise
        out[name] = jnp.asarray(drawn.astype(out[name].dtype))
    for name, factor in factors.items():
        out[name] = (out[name] * factor).astype(out[name].dtype)
    return out
```

```python
from contextlib import ExitStack

import concourse.bass as bass
from concourse import mybir

F32 = mybir.dt.float32
F32R = mybir.dt.float32r
BF16 = mybir.dt.bfloat16
ALU = mybir.AluOpType
ACT = mybir.ActivationFunctionType

B, N, D = 64, 128, 256
PG = 2
PAIRS = B // PG
C = D // 128
SLOPE = 0.2
ROW_EPS = 1e-12
LN_EPS = 1e-5
UNROLL = 4
LAGS = 4
W_COLS = 3 * D + 4
Z_COLS = D + 4
V_COLS = D + 2
VS_COLS = V_COLS + N


class Pair:

    def __init__(self, base, shift):
        self.base, self.shift = base, shift

    def exists(self):
        return not isinstance(self.base, int) or 0 <= self.base + self.shift < PAIRS

    def slot(self, ring):
        return (self.base + self.shift if isinstance(self.base, int) else self.shift) % ring

    def index(self):
        return self.base + self.shift

    def count(self, per_pair, extra):
        if isinstance(self.base, int):
            return per_pair * (self.base + self.shift) + extra
        return self.base * per_pair + (per_pair * self.shift + extra)

    def turns(self, ring, extra):
        whole = 16 * (self.shift // ring + extra) if not isinstance(self.base, int) else None
        if whole is None:
            return 16 * ((self.base + self.shift) // ring + extra)
        return self.base * (16 // ring) + whole

    def has(self, before):
        return not isinstance(self.base, int) or self.base + self.shift - before >= 0


def run_steps(engine, step):
    for p in range(UNROLL):
        step([Pair(0, p - lag) for lag in range(LAGS + 1)])
    with engine.Fori(UNROLL, PAIRS, UNROLL) as i:
        for k in range(UNROLL):
            step([Pair(i, k - lag) for lag in range(LAGS + 1)])
    for p in range(PAIRS, PAIRS + LAGS):
        step([Pair(0, p - lag) for lag in range(LAGS + 1)])


def wait(engine, sem, value):
    if not isinstance(value, int) or value > 0:
        engine.wait_ge(sem, value)


def two_layer_graph_kernel(nc, x, xt, adjt, columns, Wv0t, ab, Wk0, bk0, Wq1, Wk1, Wv1t, bv1, out):
    with ExitStack() as ctx:
        def sb(name, shape, dt=F32):
            return ctx.enter_context(nc.sbuf_tensor(name, shape, dt))

        def psum(name, shape):
            return ctx.enter_context(nc.psum_tensor(name, shape, F32))

        def sem(name):
            return ctx.enter_context(nc.semaphore(name))

        w_raw = sb("w_raw", [128, C, W_COLS])
        w_hi, w_lo = (sb(n, [128, C, W_COLS], F32R) for n in ("w_hi", "w_lo"))
        wv0t_raw = sb("wv0t_raw", [128, C, D])
        wq1_raw = sb("wq1_raw", [128, C, D])
        wk1_raw = sb("wk1_raw", [128, C, D])
        v_raw = sb("v_raw", [128, C, V_COLS])
        m_hi, m_lo = (sb(n, [128, C, D], F32R) for n in ("m_hi", "m_lo"))
        cols = sb("cols", [128, C, 5])
        ab_all = sb("ab_all", [128, 1])
        s_const = sb("s_const", [128, 4])
        u_col = sb("u_col", [128, C])
        c_const = sb("c_const", [128, 1])
        bv_all = sb("bv_all", [128, D])
        adds_raw = sb("adds_raw", [128, 2, D])
        adds_rest = sb("adds_rest", [128, 2, D])
        adds_hi, adds_mid, adds_low, adds = (
            sb(n, [128, 2, D], BF16) for n in ("adds_hi", "adds_mid", "adds_low", "adds"))
        ones_bf = sb("ones_bf", [128, 128], BF16)
        ones = sb("ones", [128, 128])
        ident = sb("ident", [128, 128])
        minus_half = sb("minus_half", [128, PG])

        xt_in = sb("xt_in", [128, 4, C, PG, N])
        x_in = sb("x_in", [128, 4, PG, D])
        adjt_in = sb("adjt_in", [128, 4, PG, N])
        y_out = sb("y_out", [128, 2, PG, D])
        xt_hi, xt_lo = (sb(n, [128, 2, C, PG, N], F32R) for n in ("xt_hi", "xt_lo"))
        s_cols = sb("s_cols", [128, PG, 4])
        z_hi, z_lo = (sb(n, [128, 2, PG, D], F32R) for n in ("z_hi", "z_lo"))
        e_full, e_slope, e_max, alpha, row_inv, t_all = (
            sb(n, [128, PG, N]) for n in ("e_full", "e_slope", "e_max", "alpha", "row_inv", "t_all"))
        t_hi, t_lo = (sb(n, [128, PG, N], F32R) for n in ("t_hi", "t_lo"))
        u_hi, u_lo = (sb(n, [128, PG, D], F32R) for n in ("u_hi", "u_lo"))
        y1 = sb("y1", [128, PG, D])
        stats1 = sb("stats1", [128, PG, 6])
        mean_var1 = sb("mean_var1", [128, PG, 2])
        var_eps1 = sb("var_eps1", [128, PG])
        rstd1 = sb("rstd1", [128, PG])
        x1 = sb("x1", [128, PG, D])
        x1t_hi, x1t_lo = (sb(n, [128, C, PG, N], F32R) for n in ("x1t_hi", "x1t_lo"))
        gv_hi, gv_lo = (sb(n, [128, PG, C, VS_COLS], F32R) for n in ("gv_hi", "gv_lo"))
        x1_bv = sb("x1_bv", [128, 2, PG, D])
        e_score, w_all = (sb(n, [128, PG, N]) for n in ("e_score", "w_all"))
        wt_hi, wt_lo = (sb(n, [128, PG, N], F32R) for n in ("wt_hi", "wt_lo"))
        v_hi, v_lo = (sb(n, [128, PG, V_COLS], F32R) for n in ("v_hi", "v_lo"))
        e_c, den, den_inv, o_scale = (sb(n, [128, PG]) for n in ("e_c", "den", "den_inv", "o_scale"))
        y2 = sb("y2", [128, PG, D])
        stats2 = sb("stats2", [128, PG, 6])
        mean_var2 = sb("mean_var2", [128, PG, 2])
        var_eps2 = sb("var_eps2", [128, PG])
        rstd2 = sb("rstd2", [128, PG])

        hu = psum("hu", [128, 2, PG, 2 * D])
        zs = psum("zs", [128, 2 * D])
        xg = psum("xg", [128, C, PG, N])
        vo = psum("vo", [128, PG, 2 * D])
        s_spread = zs[:, 0:PG * N].rearrange("p (g n) -> p g n", g=PG)
        row_sum = s_spread

        ld_w, ld_cols, ld_m, ld_v, ld_adds = (
            sem(n) for n in ("ld_w", "ld_cols", "ld_m", "ld_v", "ld_adds"))
        consts_set, adds_zero, adds_set, ident_set = (
            sem(n) for n in ("consts_set", "adds_zero", "adds_set", "ident_set"))
        setup_mm, setup_cols, setup_hi, setup_lo, adds_split = (
            sem(n) for n in ("setup_mm", "setup_cols", "setup_hi", "setup_lo", "adds_split"))
        xt_loaded = [sem(f"xt_loaded{n}") for n in range(4)]
        x_loaded = [sem(f"x_loaded{n}") for n in range(4)]
        adjt_loaded = [sem(f"adjt_loaded{n}") for n in range(4)]
        stored = [sem(f"stored{n}") for n in range(2)]
        xt_hi_set, xt_lo_set = sem("xt_hi_set"), sem("xt_lo_set")
        z_mm, xw_mm = sem("z_mm"), sem("xw_mm")
        z_hi_set, z_lo_set = sem("z_hi_set"), sem("z_lo_set")
        s_spread_mm, e_set, e_max_set, alpha_set = (
            sem(n) for n in ("s_spread_mm", "e_set", "e_max_set", "alpha_set"))
        row_sum_mm, row_inv_set, t_set, t_hi_set, t_lo_set = (
            sem(n) for n in ("row_sum_mm", "row_inv_set", "t_set", "t_hi_set", "t_lo_set"))
        u_mm, u_hi_set, u_lo_set, h_mm = (sem(n) for n in ("u_mm", "u_hi_set", "u_lo_set", "h_mm"))
        y1_set, stats1_set, mean1_set, var1_set, rstd1_set, x1_set = (
            sem(n) for n in ("y1_set", "stats1_set", "mean1_set", "var1_set", "rstd1_set", "x1_set"))
        x1t_mm, x1t_hi_set, x1t_lo_set = (sem(n) for n in ("x1t_mm", "x1t_hi_set", "x1t_lo_set"))
        g_mm, g_hi_set, g_lo_set, x1_bv_set = (
            sem(n) for n in ("g_mm", "g_hi_set", "g_lo_set", "x1_bv_set"))
        vs_mm, vs_read, v_lo_set, w_set, wt_hi_set, wt_lo_set = (
            sem(n) for n in ("vs_mm", "vs_read", "v_lo_set", "w_set", "wt_hi_set", "wt_lo_set"))
        o_mm, den_set, den_inv_set, o_scale_set, y2_set = (
            sem(n) for n in ("o_mm", "den_set", "den_inv_set", "o_scale_set", "y2_set"))
        stats2_set, mean2_set, var2_set, rstd2_set, y_out_set = (
            sem(n) for n in ("stats2_set", "mean2_set", "var2_set", "rstd2_set", "y_out_set"))

        by_chunk = "(c p) n -> p c n"
        block = ctx.enter_context(nc.Block())

        @block.sync
        def _(sp):
            def load(q):
                if q.has(4):
                    sp.wait_ge(xt_lo_set, q.count(1, -3))
                sp.dma_start(xt_in[:, q.slot(4)], xt[q.index()]).then_inc(xt_loaded[q.slot(4)], 16)
                if q.has(4):
                    sp.wait_ge(y1_set, q.count(1, -3))
                sp.dma_start(x_in[:, q.slot(4)], x[q.index()]).then_inc(x_loaded[q.slot(4)], 16)
                if q.has(4):
                    sp.wait_ge(w_set, q.count(1, -3))
                sp.dma_start(adjt_in[:, q.slot(4)], adjt[q.index()]).then_inc(adjt_loaded[q.slot(4)], 16)

            def store(q):
                sp.wait_ge(y_out_set, q.count(1, 1))
                sp.dma_start(out[q.index()], y_out[:, q.slot(2)]).then_inc(stored[q.slot(2)], 16)

            for n in range(UNROLL + 1):
                load(Pair(0, n))
            with sp.Fori(0, PAIRS - UNROLL - 4, UNROLL) as i:
                for k in range(UNROLL):
                    load(Pair(i, k + UNROLL + 1))
                    store(Pair(i, k))
            for n in range(PAIRS - UNROLL - 4, PAIRS):
                if n + UNROLL + 1 < PAIRS:
                    load(Pair(0, n + UNROLL + 1))
                store(Pair(0, n))
            for n in range(2):
                sp.wait_ge(stored[n], 16 * (PAIRS // 2 + 1))

        @block.gpsimd
        def _(pool):
            nc.gpsimd.memset(adds_raw[:], 0.0).then_inc(adds_zero, 1)
            nc.gpsimd.memset(ident[:], 0.0).then_inc(ident_set, 1)
            nc.gpsimd.memset(ones[:], 1.0).then_inc(consts_set, 1)
            nc.gpsimd.memset(ones_bf[:], 1.0).then_inc(consts_set, 1)
            nc.gpsimd.memset(minus_half[:], -0.5).then_inc(consts_set, 1)
            pool.wait_ge(ident_set, 1)
            nc.gpsimd.affine_select(out=ident[:], in_=ident[:], compare_op=ALU.not_equal, fill=1.0, base=0,
                                    pattern=[[-1, 128]], channel_multiplier=1).then_inc(ident_set, 1)
            pool.wait_ge(consts_set, 3)

            def step(q):
                q0, q1, q2, q3, q4 = q
                if q4.exists():
                    pool.wait_ge(vs_read, q4.count(2, 2))
                    nc.gpsimd.tensor_tensor(w_all[:], adjt_in[:, q4.slot(4)], e_score[:], ALU.mult).then_inc(w_set, 1)
                    pool.wait_ge(wt_hi_set, q4.count(1, 1))
                    pool.wait_ge(w_set, q4.count(1, 1))
                    nc.gpsimd.tensor_tensor(wt_lo[:], w_all[:], wt_hi[:].bitcast(F32), ALU.subtract).then_inc(wt_lo_set, 1)
                if q0.exists():
                    pool.wait_ge(xt_hi_set, q0.count(1, 1))
                    if q0.has(2):
                        wait(pool, xw_mm, q0.count(1, -1))
                    nc.gpsimd.tensor_tensor(xt_lo[:, q0.slot(2)], xt_in[:, q0.slot(4)],
                                            xt_hi[:, q0.slot(2)].bitcast(F32), ALU.subtract).then_inc(xt_lo_set, 1)
                if q3.exists():
                    if not q3.has(1):
                        pool.wait_ge(ld_v, 32)
                    pool.wait_ge(x1_set, q3.count(1, 1))
                    if q3.has(2):
                        wait(pool, y2_set, q3.count(1, -1))
                    for g in range(PG):
                        last = nc.gpsimd.tensor_tensor(x1_bv[:, q3.slot(2), g], x1[:, g], bv_all[:], ALU.add)
                    last.then_inc(x1_bv_set, 1)
                if q4.exists():
                    pool.wait_ge(var2_set, q4.count(1, 1))
                    nc.gpsimd.tensor_tensor(rstd2[:], var_eps2[:], minus_half[:], ALU.pow).then_inc(rstd2_set, 1)
                if q1.exists():
                    pool.wait_ge(e_max_set, q1.count(1, 1))
                    pool.wait_ge(adjt_loaded[q1.slot(4)], q1.turns(4, 1))
                    wait(pool, t_set, q1.count(1, 0))
                    nc.gpsimd.tensor_tensor(alpha[:], adjt_in[:, q1.slot(4)], e_max[:], ALU.mult).then_inc(alpha_set, 1)
                if q2.exists():
                    pool.wait_ge(var1_set, q2.count(1, 1))
                    wait(pool, x1_set, q2.count(1, 0))
                    nc.gpsimd.tensor_tensor(rstd1[:], var_eps1[:], minus_half[:], ALU.pow).then_inc(rstd1_set, 1)

            run_steps(pool, step)

        @block.scalar
        def _(act):
            for n, k in ((1, 0), (0, 1), (2, 2)):
                act.dma_start(w_raw[:, :, k * D:(k + 1) * D], Wk0[n].rearrange(by_chunk, p=128)).then_inc(ld_w, 16)
            act.dma_start(cols[:], columns).then_inc(ld_cols, 16)
            act.dma_start(wv0t_raw[:], Wv0t.rearrange(by_chunk, p=128)).then_inc(ld_cols, 16)
            act.dma_start(ab_all[:], ab.partition_broadcast(128)).then_inc(ld_cols, 16)
            act.dma_start(wq1_raw[:], Wq1.rearrange(by_chunk, p=128)).then_inc(ld_m, 16)
            act.dma_start(wk1_raw[:], Wk1.rearrange(by_chunk, p=128)).then_inc(ld_m, 16)
            act.wait_ge(adds_zero, 1)
            for r in (0, 32, 64):
                act.dma_start(adds_raw[r:r + 3, 0, :], bk0).then_inc(ld_adds, 16)
            act.dma_start(v_raw[:, :, 0:D], Wv1t.rearrange(by_chunk, p=128)).then_inc(ld_v, 16)
            act.dma_start(bv_all[:], bv1.partition_broadcast(128)).then_inc(ld_v, 16)

            act.wait_ge(ld_w, 48)
            act.wait_ge(setup_cols, 2)
            nc.scalar.copy(w_hi[:], w_raw[:]).then_inc(setup_hi, 1)
            act.wait_ge(setup_mm, 2)
            nc.scalar.copy(m_hi[:], hu[:, 0, 0, :].rearrange("p (c n) -> p c n", c=C)).then_inc(setup_hi, 1)
            act.wait_ge(setup_cols, 4)
            for g in range(PG):
                nc.scalar.copy(gv_hi[:, g, :, 0:V_COLS], v_raw[:]).then_inc(setup_hi, 1)

            def step(q):
                q0, q1, q2, q3, q4 = q
                if q3.exists():
                    act.wait_ge(x1t_mm, q3.count(1, 1))
                    nc.scalar.copy(x1t_hi[:], xg[:]).then_inc(x1t_hi_set, 1)
                if q4.exists():
                    act.wait_ge(w_set, q4.count(1, 1))
                    nc.scalar.copy(wt_hi[:], w_all[:]).then_inc(wt_hi_set, 1)
                if q2.exists():
                    act.wait_ge(t_set, q2.count(1, 1))
                    nc.scalar.copy(t_hi[:], t_all[:]).then_inc(t_hi_set, 1)

                def split_z(g):
                    act.wait_ge(z_mm, q1.count(2, 1 + g))
                    if q1.has(2):
                        wait(act, u_mm, q1.count(1, -1))
                    nc.scalar.copy(z_hi[:, q1.slot(2), g], zs[:, 0:D]).then_inc(z_hi_set, 1)

                if q1.exists():
                    split_z(0)
                if q2.exists():
                    act.wait_ge(u_mm, q2.count(1, 1))
                    nc.scalar.copy(u_hi[:], hu[:, q2.slot(2), :, 0:D]).then_inc(u_hi_set, 1)
                if q3.exists():
                    act.wait_ge(g_mm, q3.count(1, 1))
                    for c in range(C):
                        last = nc.scalar.activation(gv_hi[:, :, c, V_COLS:], xg[:, c], ACT.Identity,
                                                    bias=u_col[:, c:c + 1])
                    last.then_inc(g_hi_set, 1)
                if q1.exists():
                    split_z(1)
                if q0.exists():
                    act.wait_ge(xt_loaded[q0.slot(4)], q0.turns(4, 1))
                    if q0.has(2):
                        wait(act, xw_mm, q0.count(1, -1))
                    nc.scalar.copy(xt_hi[:, q0.slot(2)], xt_in[:, q0.slot(4)]).then_inc(xt_hi_set, 1)
                if q1.exists():
                    act.wait_ge(s_spread_mm, q1.count(1, 1))
                    wait(act, e_max_set, q1.count(1, 0))
                    for g in range(PG):
                        nc.scalar.activation(e_full[:, g], s_spread[:, g], ACT.Exp, bias=s_cols[:, g, 0:1])
                        last = nc.scalar.activation(e_slope[:, g], s_spread[:, g], ACT.Exp,
                                                    bias=s_cols[:, g, 2:3], scale=SLOPE)
                    last.then_inc(e_set, 1)
                if q3.exists():
                    for g in range(PG):
                        act.wait_ge(vs_mm, q3.count(2, 1 + g))
                        if g == 0:
                            wait(act, w_set, q3.count(1, 0))
                        nc.scalar.activation(e_score[:, g], vo[:, g, V_COLS:VS_COLS], ACT.Exp)
                        nc.scalar.activation(e_c[:, g:g + 1], vo[:, g, D:D + 1], ACT.Exp, bias=c_const[:])
                        nc.scalar.copy(v_hi[:, g, 0:D], vo[:, g, 0:D]).then_inc(vs_read, 1)

            act.wait_ge(setup_lo, 1)
            run_steps(act, step)

        @block.vector
        def _(dve):
            nc.vector.memset(w_raw[:, :, W_COLS - 1:W_COLS], 0.0).then_inc(stored[1], 16)
            nc.vector.memset(v_raw[:, :, V_COLS - 1:V_COLS], 0.0).then_inc(stored[0], 16)
            nc.vector.memset(v_hi[:, :, D:D + 1].bitcast(F32), 1.0)
            nc.vector.memset(v_hi[:, :, D + 1:D + 2].bitcast(F32), 0.0)
            nc.vector.memset(v_lo[:, :, D:D + 2].bitcast(F32), 0.0)
            nc.vector.memset(s_const[:, 3:4], 0.0).then_inc(setup_cols, 1)

            dve.wait_ge(adds_zero, 1)
            for r in (0, 32, 64):
                nc.vector.memset(adds_raw[r:r + 1, 1, :], ROW_EPS).then_inc(adds_set, 1)

            small, small1 = hu[:, 1, 0, :], hu[:, 1, 1, :]
            dve.wait_ge(setup_mm, 1)
            wji = small[:, 0:2 * C].rearrange("p (c n) -> p c n", n=2)
            nc.vector.tensor_copy(w_raw[:, :, 3 * D:3 * D + 2], wji)
            nc.vector.tensor_scalar(w_raw[:, :, 3 * D + 2:3 * D + 3], wji[:, :, 0:1], SLOPE, None,
                                    ALU.mult).then_inc(setup_cols, 1)
            dve.wait_ge(ld_cols, 48)
            nc.vector.tensor_scalar(s_const[:, 0:1], small[:, 8:9], ab_all[:], None, ALU.add)
            nc.vector.tensor_scalar(s_const[:, 2:3], small[:, 8:9], ab_all[:], SLOPE, ALU.add, ALU.mult)
            nc.vector.tensor_copy(s_const[:, 1:2], small[:, 9:10])
            dve.wait_ge(setup_mm, 3)
            nc.vector.tensor_copy(u_col[:], small1[:, 16:16 + C])
            nc.vector.tensor_copy(c_const[:], small1[:, 24:25]).then_inc(setup_cols, 1)
            dve.wait_ge(ld_v, 32)
            nc.vector.tensor_copy(v_raw[:, :, D:D + 1],
                                  small1[:, 20:20 + C].rearrange("p (c n) -> p c n", n=1)).then_inc(setup_cols, 1)
            dve.wait_ge(setup_hi, 1)
            nc.vector.tensor_tensor(w_lo[:], w_raw[:], w_hi[:].bitcast(F32), ALU.subtract).then_inc(setup_lo, 1)
            dve.wait_ge(setup_hi, 2)
            nc.vector.tensor_tensor(m_lo[:], hu[:, 0, 0, :].rearrange("p (c n) -> p c n", c=C),
                                    m_hi[:].bitcast(F32), ALU.subtract).then_inc(setup_lo, 1)
            dve.wait_ge(setup_hi, 2 + PG)
            for g in range(PG):
                nc.vector.tensor_tensor(gv_lo[:, g, :, 0:V_COLS], v_raw[:], gv_hi[:, g, :, 0:V_COLS].bitcast(F32),
                                        ALU.subtract).then_inc(setup_lo, 1)
            dve.wait_ge(ld_adds, 48)
            dve.wait_ge(adds_set, 3)
            nc.vector.tensor_copy(adds_hi[:], adds_raw[:]).then_inc(adds_split, 1)
            dve.wait_ge(adds_split, 1)
            nc.vector.tensor_tensor(adds_rest[:], adds_raw[:], adds_hi[:], ALU.subtract).then_inc(adds_split, 1)
            dve.wait_ge(adds_split, 2)
            nc.vector.tensor_copy(adds_mid[:], adds_rest[:]).then_inc(adds_split, 1)
            dve.wait_ge(adds_split, 3)
            nc.vector.tensor_tensor(adds_low[:], adds_rest[:], adds_mid[:], ALU.subtract).then_inc(adds_split, 1)
            dve.wait_ge(adds_split, 4)
            nc.vector.tensor_copy(adds[0:32], adds_hi[0:32]).then_inc(adds_split, 1)
            nc.vector.tensor_copy(adds[32:64], adds_mid[32:64]).then_inc(adds_split, 1)
            nc.vector.tensor_copy(adds[64:128], adds_low[64:128]).then_inc(adds_split, 1)

            def step(q):
                q0, q1, q2, q3, q4 = q
                if q3.exists():
                    dve.wait_ge(x1t_hi_set, q3.count(1, 1))
                    nc.vector.tensor_tensor(x1t_lo[:], xg[:], x1t_hi[:].bitcast(F32), ALU.subtract).then_inc(x1t_lo_set, 1)
                if q2.exists():
                    dve.wait_ge(t_hi_set, q2.count(1, 1))
                    nc.vector.tensor_tensor(t_lo[:], t_all[:], t_hi[:].bitcast(F32), ALU.subtract).then_inc(t_lo_set, 1)

                def split_z(g):
                    dve.wait_ge(z_hi_set, q1.count(2, 1 + g))
                    nc.vector.tensor_tensor(s_cols[:, g], zs[:, D:Z_COLS], s_const[:], ALU.add)
                    nc.vector.tensor_tensor(z_lo[:, q1.slot(2), g], zs[:, 0:D], z_hi[:, q1.slot(2), g].bitcast(F32),
                                            ALU.subtract).then_inc(z_lo_set, 1)

                if q1.exists():
                    split_z(0)
                if q2.exists():
                    dve.wait_ge(u_hi_set, q2.count(1, 1))
                    nc.vector.tensor_tensor(u_lo[:], hu[:, q2.slot(2), :, 0:D], u_hi[:].bitcast(F32),
                                            ALU.subtract).then_inc(u_lo_set, 1)
                if q3.exists():
                    dve.wait_ge(g_hi_set, q3.count(1, 1))
                    for c in range(C):
                        last = nc.vector.scalar_tensor_tensor(
                            out=gv_lo[:, :, c, V_COLS:], in0=xg[:, c], scalar=u_col[:, c:c + 1],
                            in1=gv_hi[:, :, c, V_COLS:].bitcast(F32), op0=ALU.add, op1=ALU.subtract)
                    last.then_inc(g_lo_set, 1)
                if q4.exists():
                    dve.wait_ge(o_mm, q4.count(1, 1))
                    nc.vector.tensor_tensor(den[:], vo[:, :, D], e_c[:], ALU.mult).then_inc(den_set, 1)
                    dve.wait_ge(den_set, q4.count(1, 1))
                    nc.vector.reciprocal(den_inv[:], den[:]).then_inc(den_inv_set, 1)
                    dve.wait_ge(den_inv_set, q4.count(1, 1))
                    nc.vector.tensor_tensor(o_scale[:], den_inv[:], e_c[:], ALU.mult).then_inc(o_scale_set, 1)
                    dve.wait_ge(x1_bv_set, q4.count(1, 1))
                    dve.wait_ge(o_scale_set, q4.count(1, 1))
                    for g in range(PG):
                        last = nc.vector.scalar_tensor_tensor(
                            out=y2[:, g], in0=vo[:, g, 0:D], scalar=o_scale[:, g:g + 1],
                            in1=x1_bv[:, q4.slot(2), g], op0=ALU.mult, op1=ALU.add)
                    last.then_inc(y2_set, 1)
                    dve.wait_ge(y2_set, q4.count(1, 1))
                    for g in range(PG):
                        last = nc.vector.bn_stats(stats2[:, g], y2[:, g])
                    last.then_inc(stats2_set, 1)
                    dve.wait_ge(stats2_set, q4.count(1, 1))
                if q1.exists():
                    split_z(1)
                if q4.exists():
                    for g in range(PG):
                        last = nc.vector.bn_aggr(mean_var2[:, g], stats2[:, g])
                    last.then_inc(mean2_set, 1)
                    dve.wait_ge(mean2_set, q4.count(1, 1))
                    nc.vector.tensor_scalar(var_eps2[:], mean_var2[:, :, 1], LN_EPS, None, ALU.add).then_inc(var2_set, 1)
                if q2.exists():
                    dve.wait_ge(h_mm, q2.count(1, 1))
                    dve.wait_ge(x_loaded[q2.slot(4)], q2.turns(4, 1))
                    nc.vector.scalar_tensor_tensor(out=y1[:], in0=hu[:, q2.slot(2), :, D:2 * D], scalar=0.0,
                                                   in1=x_in[:, q2.slot(4)], op0=ALU.max, op1=ALU.add).then_inc(y1_set, 1)
                    dve.wait_ge(y1_set, q2.count(1, 1))
                    for g in range(PG):
                        last = nc.vector.bn_stats(stats1[:, g], y1[:, g])
                    last.then_inc(stats1_set, 1)
                    dve.wait_ge(stats1_set, q2.count(1, 1))
                if q1.exists():
                    wait(dve, alpha_set, q1.count(1, 0))
                    dve.wait_ge(e_set, q1.count(1, 1))
                    nc.vector.tensor_tensor(e_max[:], e_full[:], e_slope[:], ALU.max).then_inc(e_max_set, 1)
                if q2.exists():
                    for g in range(PG):
                        last = nc.vector.bn_aggr(mean_var1[:, g], stats1[:, g])
                    last.then_inc(mean1_set, 1)
                    dve.wait_ge(mean1_set, q2.count(1, 1))
                    nc.vector.tensor_scalar(var_eps1[:], mean_var1[:, :, 1], LN_EPS, None, ALU.add).then_inc(var1_set, 1)
                if q4.exists():
                    dve.wait_ge(rstd2_set, q4.count(1, 1))
                    dve.wait_ge(stored[q4.slot(2)], q4.turns(2, 1))
                    for g in range(PG):
                        last = nc.vector.tensor_scalar(y_out[:, q4.slot(2), g], y2[:, g], mean_var2[:, g, 0:1],
                                                       rstd2[:, g:g + 1], ALU.subtract, ALU.mult)
                    last.then_inc(y_out_set, 1)
                if q2.exists():
                    dve.wait_ge(rstd1_set, q2.count(1, 1))
                    wait(dve, x1_bv_set, q2.count(1, 0))
                    for g in range(PG):
                        last = nc.vector.tensor_scalar(x1[:, g], y1[:, g], mean_var1[:, g, 0:1],
                                                       rstd1[:, g:g + 1], ALU.subtract, ALU.mult)
                    last.then_inc(x1_set, 1)
                if q3.exists():
                    for g in range(PG):
                        dve.wait_ge(vs_read, q3.count(2, 1 + g))
                        last = nc.vector.tensor_tensor(v_lo[:, g, 0:D], vo[:, g, 0:D], v_hi[:, g, 0:D].bitcast(F32),
                                                       ALU.subtract)
                    last.then_inc(v_lo_set, 1)
                if q1.exists():
                    dve.wait_ge(row_sum_mm, q1.count(1, 1))
                    nc.vector.reciprocal(row_inv[:], row_sum).then_inc(row_inv_set, 1)
                    dve.wait_ge(row_inv_set, q1.count(1, 1))
                    nc.vector.tensor_tensor(t_all[:], alpha[:], row_inv[:], ALU.mult).then_inc(t_set, 1)

            run_steps(dve, step)

        @block.tensor
        def _(pe):
            mm = nc.tensor.matmul

            def split_product(to, stationary, moving, start, stop):
                terms = [(s[i], m[j]) for s, m in zip(stationary, moving) for i, j in ((0, 0), (0, 1), (1, 0))]
                for n, (s, m) in enumerate(terms):
                    last = mm(to, s, m, start=start and n == 0, stop=stop and n == len(terms) - 1,
                              skip_group_check=True)
                return last

            small, small1 = hu[:, 1, 0, :], hu[:, 1, 1, :]
            pe.wait_ge(ld_cols, 48)
            for c in range(C):
                for o in range(C):
                    last = mm(small[:, 2 * c:2 * c + 2], wv0t_raw[:, o, c * 128:(c + 1) * 128], cols[:, o, 0:2],
                              start=(o == 0), stop=(o == C - 1))
            for o in range(C):
                last = mm(small[:, 8:10], cols[:, o, 2:3].to_broadcast([128, 128]), cols[:, o, 0:2],
                          start=(o == 0), stop=(o == C - 1))
            last.then_inc(setup_mm, 1)
            pe.wait_ge(ld_m, 32)
            for c in range(C):
                for o in range(C):
                    last = mm(hu[:, 0, 0, c * D:(c + 1) * D], wq1_raw[:, o, c * 128:(c + 1) * 128], wk1_raw[:, o, :],
                              start=(o == 0), stop=(o == C - 1))
            last.then_inc(setup_mm, 1)
            for c in range(C):
                for o in range(C):
                    mm(small1[:, 16 + c:17 + c], wk1_raw[:, o, c * 128:(c + 1) * 128], cols[:, o, 3:4],
                       start=(o == 0), stop=(o == C - 1))
                for o in range(C):
                    mm(small1[:, 20 + c:21 + c], wq1_raw[:, o, c * 128:(c + 1) * 128], cols[:, o, 4:5],
                       start=(o == 0), stop=(o == C - 1))
            for o in range(C):
                last = mm(small1[:, 24:25], cols[:, o, 3:4].to_broadcast([128, 128]), cols[:, o, 4:5],
                          start=(o == 0), stop=(o == C - 1))
            last.then_inc(setup_mm, 1)
            pe.wait_ge(ident_set, 2)
            pe.wait_ge(consts_set, 3)
            pe.wait_ge(adds_split, 7)
            pe.wait_ge(setup_lo, 2 + PG)

            def weights(lo, hi):
                return [(w_hi[:, c, lo:hi], w_lo[:, c, lo:hi]) for c in range(C)]

            def step(q):
                q0, q1, q2, q3, q4 = q

                def xt_of(g):
                    return [(xt_hi[:, q1.slot(2), c, g], xt_lo[:, q1.slot(2), c, g]) for c in range(C)]

                if q1.exists():
                    pe.wait_ge(xt_lo_set, q1.count(1, 1))
                    if q1.has(2):
                        wait(pe, y1_set, q1.count(1, -1))
                    split_product(hu[:, q1.slot(2), 0], xt_of(0), weights(0, 2 * D), True, False)
                    wait(pe, row_inv_set, q1.count(1, 0))
                    split_product(zs[:, 0:Z_COLS], xt_of(0), weights(2 * D, W_COLS), True, True).then_inc(z_mm, 1)
                if q2.exists():
                    pe.wait_ge(t_lo_set, q2.count(1, 1))
                    pe.wait_ge(z_lo_set, q2.count(2, 2))
                    for g in range(PG):
                        last = split_product(hu[:, q2.slot(2), g, 0:D], [(t_hi[:, g], t_lo[:, g])],
                                             [(z_hi[:, q2.slot(2), g], z_lo[:, q2.slot(2), g])], False, False)
                    last.then_inc(u_mm, 1)
                if q3.exists():
                    pe.wait_ge(x1t_lo_set, q3.count(1, 1))
                    for c in range(C):
                        last = split_product(
                            xg[:, c], [(m_hi[:, k, c * 128:(c + 1) * 128], m_lo[:, k, c * 128:(c + 1) * 128])
                                       for k in range(C)],
                            [(x1t_hi[:, k], x1t_lo[:, k]) for k in range(C)], True, True)
                    last.then_inc(g_mm, 1)
                if q4.exists():
                    pe.wait_ge(wt_lo_set, q4.count(1, 1))
                    pe.wait_ge(v_lo_set, q4.count(1, 1))
                    for g in range(PG):
                        last = split_product(vo[:, g, 0:V_COLS], [(wt_hi[:, g], wt_lo[:, g])],
                                             [(v_hi[:, g], v_lo[:, g])], True, True)
                    last.then_inc(o_mm, 1)
                if q1.exists():
                    pe.wait_ge(z_lo_set, q1.count(2, 1))
                    split_product(zs[:, 0:Z_COLS], xt_of(1), weights(2 * D, W_COLS), True, True).then_inc(z_mm, 1)
                    split_product(hu[:, q1.slot(2), 1], xt_of(1), weights(0, 2 * D), True, False).then_inc(xw_mm, 1)
                if q2.exists():
                    pe.wait_ge(u_lo_set, q2.count(1, 1))
                    for g in range(PG):
                        mm(hu[:, q2.slot(2), g, D:2 * D], ones_bf[:], adds[:, 0], start=False, stop=False,
                           skip_group_check=True)
                        last = split_product(hu[:, q2.slot(2), g, D:2 * D], [(t_hi[:, g], t_lo[:, g])],
                                             [(u_hi[:, g], u_lo[:, g])], False, True)
                    last.then_inc(h_mm, 1)
                if q1.exists():
                    pe.wait_ge(z_lo_set, q1.count(2, 2))
                    for g in range(PG):
                        last = nc.tensor.transpose(s_spread[:, g], s_cols[:, g, 1:2].to_broadcast([128, N]), ident[:])
                    last.then_inc(s_spread_mm, 1)
                if q3.exists():
                    pe.wait_ge(g_lo_set, q3.count(1, 1))
                    wait(pe, y2_set, q3.count(1, 0))
                    for g in range(PG):
                        split_product(vo[:, g, 0:VS_COLS], [(x1t_hi[:, c, g], x1t_lo[:, c, g]) for c in range(C)],
                                      [(gv_hi[:, g, c], gv_lo[:, g, c]) for c in range(C)],
                                      True, True).then_inc(vs_mm, 1)
                if q1.exists():
                    pe.wait_ge(alpha_set, q1.count(1, 1))
                    mm(row_sum, ones[:], alpha[:], start=True, stop=False, skip_group_check=True)
                    mm(row_sum, ones_bf[:], adds[:, 1], start=False, stop=True,
                       skip_group_check=True).then_inc(row_sum_mm, 1)
                if q2.exists():
                    pe.wait_ge(x1_set, q2.count(1, 1))
                    wait(pe, g_lo_set, q2.count(1, 0))
                    for g in range(PG):
                        for c in range(C):
                            last = nc.tensor.transpose(xg[:, c, g], x1[:, g, c * 128:(c + 1) * 128], ident[:])
                    last.then_inc(x1t_mm, 1)

            run_steps(pe, step)


def kernel(**inputs):
    import numpy as np
    import concourse.bacc as bacc
    from concourse.bass_utils import run_bass_kernel_spmd

    a = {k: np.asarray(v) for k, v in inputs.items()}
    x, adj = a["x"], a["adj"]
    aw = a["L0_gnn_aw"][:, 0]
    columns = np.stack([aw[:D], aw[D:], a["L0_gnn_bv"], a["L1_gnn_Wq_b"], a["L1_gnn_Wk_b"]], axis=-1)
    arrays = {
        "x": x.reshape(PAIRS, PG, N, D).transpose(0, 2, 1, 3),
        "xt": x.reshape(PAIRS, PG, N, C, 128).transpose(0, 4, 3, 1, 2),
        "adjt": adj.reshape(PAIRS, PG, N, N).transpose(0, 3, 1, 2),
        "columns": columns.reshape(C, 128, 5).transpose(1, 0, 2),
        "Wv0t": a["L0_gnn_Wv"].T,
        "ab": a["L0_gnn_ab"],
        "Wk0": a["L0_gnn_Wk"],
        "bk0": a["L0_gnn_bk"],
        "Wq1": a["L1_gnn_Wq_w"],
        "Wk1": a["L1_gnn_Wk_w"],
        "Wv1t": a["L1_gnn_Wv_w"].T,
        "bv1": a["L1_gnn_Wv_b"],
    }
    nc = bacc.Bacc("TRN2", target_bir_lowering=False, num_devices=1)
    feed, args = {}, []
    for name, value in arrays.items():
        value = np.ascontiguousarray(value)
        feed[f"in_{name}"] = value
        args.append(nc.dram_tensor(f"in_{name}", value.shape, F32, kind="ExternalInput").ap())
    args.append(nc.dram_tensor("out", (PAIRS, N, PG, D), F32, kind="ExternalOutput").ap())
    two_layer_graph_kernel(nc, *args)
    result = run_bass_kernel_spmd(nc, [feed], core_ids=[0]).results[0]["out"]
    return np.ascontiguousarray(result.transpose(0, 2, 1, 3).reshape(B, N, D))
```

```python
from contextlib import ExitStack

import concourse.bass as bass
from concourse import mybir

F32 = mybir.dt.float32
F32R = mybir.dt.float32r
BF16 = mybir.dt.bfloat16
ALU = mybir.AluOpType
ACT = mybir.ActivationFunctionType

B, N, D = 64, 128, 256
PG = 2
PAIRS = B // PG
C = D // 128
SLOPE = 0.2
ROW_EPS = 1e-12
LN_EPS = 1e-5
UNROLL = 4
LAGS = 4
W_COLS = 3 * D + 4
Z_COLS = D + 4
V_COLS = D + 2
VS_COLS = V_COLS + N


class Pair:

    def __init__(self, base, shift):
        self.base, self.shift = base, shift

    def exists(self):
        return not isinstance(self.base, int) or 0 <= self.base + self.shift < PAIRS

    def slot(self, ring):
        return (self.base + self.shift if isinstance(self.base, int) else self.shift) % ring

    def index(self):
        return self.base + self.shift

    def count(self, per_pair, extra):
        if isinstance(self.base, int):
            return per_pair * (self.base + self.shift) + extra
        return self.base * per_pair + (per_pair * self.shift + extra)

    def turns(self, ring, extra):
        whole = 16 * (self.shift // ring + extra) if not isinstance(self.base, int) else None
        if whole is None:
            return 16 * ((self.base + self.shift) // ring + extra)
        return self.base * (16 // ring) + whole

    def has(self, before):
        return not isinstance(self.base, int) or self.base + self.shift - before >= 0


def run_steps(engine, step):
    for p in range(UNROLL):
        step([Pair(0, p - lag) for lag in range(LAGS + 1)])
    with engine.Fori(UNROLL, PAIRS, UNROLL) as i:
        for k in range(UNROLL):
            step([Pair(i, k - lag) for lag in range(LAGS + 1)])
    for p in range(PAIRS, PAIRS + LAGS):
        step([Pair(0, p - lag) for lag in range(LAGS + 1)])


def wait(engine, sem, value):
    if not isinstance(value, int) or value > 0:
        engine.wait_ge(sem, value)


def two_layer_graph_kernel(nc, x, xt, adjt, columns, Wv0t, ab, Wk0, bk0, Wq1, Wk1, Wv1t, bv1, out):
    with ExitStack() as ctx:
        def sb(name, shape, dt=F32):
            return ctx.enter_context(nc.sbuf_tensor(name, shape, dt))

        def psum(name, shape):
            return ctx.enter_context(nc.psum_tensor(name, shape, F32))

        def sem(name):
            return ctx.enter_context(nc.semaphore(name))

        w_raw = sb("w_raw", [128, C, W_COLS])
        w_hi, w_lo = (sb(n, [128, C, W_COLS], F32R) for n in ("w_hi", "w_lo"))
        wv0t_raw = sb("wv0t_raw", [128, C, D])
        wq1_raw = sb("wq1_raw", [128, C, D])
        wk1_raw = sb("wk1_raw", [128, C, D])
        v_raw = sb("v_raw", [128, C, V_COLS])
        m_hi, m_lo = (sb(n, [128, C, D], F32R) for n in ("m_hi", "m_lo"))
        cols = sb("cols", [128, C, 5])
        ab_all = sb("ab_all", [128, 1])
        s_const = sb("s_const", [128, 4])
        u_col = sb("u_col", [128, C])
        c_const = sb("c_const", [128, 1])
        bv_all = sb("bv_all", [128, D])
        bias_raw = sb("bias_raw", [128, D])
        bias_rest = sb("bias_rest", [128, D])
        bias_hi, bias_mid, bias_low, bias_parts = (
            sb(n, [128, D], BF16) for n in ("bias_hi", "bias_mid", "bias_low", "bias_parts"))
        ones_bf = sb("ones_bf", [128, 128], BF16)
        ones_col = sb("ones_col", [128, 1])
        ident = sb("ident", [128, 128])
        minus_half = sb("minus_half", [128, PG])

        xt_in = sb("xt_in", [128, 4, C, PG, N])
        x_in = sb("x_in", [128, 4, PG, D])
        adjt_in = sb("adjt_in", [128, 4, PG, N])
        y_out = sb("y_out", [128, 2, PG, D])
        xt_hi, xt_lo = (sb(n, [128, 4, C, PG, N], F32R) for n in ("xt_hi", "xt_lo"))
        s_cols = sb("s_cols", [128, PG, 4])
        z_hi, z_lo = (sb(n, [128, PG, D], F32R) for n in ("z_hi", "z_lo"))
        e_full, e_slope, e_max, alpha, t_all = (
            sb(n, [128, PG, N]) for n in ("e_full", "e_slope", "e_max", "alpha", "t_all"))
        row_sum_eps, row_inv = (sb(n, [128, PG]) for n in ("row_sum_eps", "row_inv"))
        t_hi, t_lo = (sb(n, [128, PG, N], F32R) for n in ("t_hi", "t_lo"))
        u_hi, u_lo = (sb(n, [128, PG, D], F32R) for n in ("u_hi", "u_lo"))
        y1 = sb("y1", [128, PG, D])
        stats1 = sb("stats1", [128, PG, 6])
        mean_var1 = sb("mean_var1", [128, PG, 2])
        var_eps1, minus_mean1, rstd1, shift1 = (
            sb(n, [128, PG]) for n in ("var_eps1", "minus_mean1", "rstd1", "shift1"))
        x1 = sb("x1", [128, PG, D])
        x1t_hi, x1t_lo = (sb(n, [128, C, PG, N], F32R) for n in ("x1t_hi", "x1t_lo"))
        gv_hi, gv_lo = (sb(n, [128, PG, C, VS_COLS], F32R) for n in ("gv_hi", "gv_lo"))
        x1_bv = sb("x1_bv", [128, 2, PG, D])
        e_score, w_all = (sb(n, [128, PG, N]) for n in ("e_score", "w_all"))
        wt_hi, wt_lo = (sb(n, [128, PG, N], F32R) for n in ("wt_hi", "wt_lo"))
        v_hi, v_lo = (sb(n, [128, PG, V_COLS], F32R) for n in ("v_hi", "v_lo"))
        e_c, den, den_inv, o_scale = (sb(n, [128, PG]) for n in ("e_c", "den", "den_inv", "o_scale"))
        y2 = sb("y2", [128, PG, D])
        stats2 = sb("stats2", [128, PG, 6])
        mean_var2 = sb("mean_var2", [128, PG, 2])
        var_eps2, minus_mean2, rstd2, shift2 = (
            sb(n, [128, PG]) for n in ("var_eps2", "minus_mean2", "rstd2", "shift2"))

        z = psum("z", [128, PG, 2 * D])
        spread = psum("spread", [128, 2 * D])
        u = psum("u", [128, PG, D])
        h = psum("h", [128, PG, D])
        xg = psum("xg", [128, C, PG, N])
        vo = psum("vo", [128, PG, 2 * D])
        spread_n = spread[:, 0:PG * N].rearrange("p (g n) -> p g n", g=PG)
        row_sum = spread[:, PG * N:PG * N + PG]
        small, small1 = z[:, 0], z[:, 1]

        ld_w, ld_cols, ld_m, ld_v, ld_bias = (
            sem(n) for n in ("ld_w", "ld_cols", "ld_m", "ld_v", "ld_bias"))
        consts_set, bias_zero, ident_set = (
            sem(n) for n in ("consts_set", "bias_zero", "ident_set"))
        setup_mm, setup_cols, setup_hi, setup_lo, bias_split = (
            sem(n) for n in ("setup_mm", "setup_cols", "setup_hi", "setup_lo", "bias_split"))
        xt_loaded = [sem(f"xt_loaded{n}") for n in range(4)]
        x_loaded = [sem(f"x_loaded{n}") for n in range(4)]
        adjt_loaded = [sem(f"adjt_loaded{n}") for n in range(4)]
        stored = [sem(f"stored{n}") for n in range(2)]
        xt_hi_set, xt_lo_set = sem("xt_hi_set"), sem("xt_lo_set")
        z_mm, z_hi_set, z_lo_set = sem("z_mm"), sem("z_hi_set"), sem("z_lo_set")
        s_spread_mm, e_set, e_max_set, alpha_set = (
            sem(n) for n in ("s_spread_mm", "e_set", "e_max_set", "alpha_set"))
        row_sum_mm, row_sum_set, row_inv_set, inv_spread_mm, t_set, t_hi_set, t_lo_set = (
            sem(n) for n in ("row_sum_mm", "row_sum_set", "row_inv_set", "inv_spread_mm", "t_set",
                             "t_hi_set", "t_lo_set"))
        u_mm, u_hi_set, u_lo_set, h_mm = (sem(n) for n in ("u_mm", "u_hi_set", "u_lo_set", "h_mm"))
        y1_set, stats1_set, mean1_set, var1_set, rstd1_set, shift1_set, x1_set = (
            sem(n) for n in ("y1_set", "stats1_set", "mean1_set", "var1_set", "rstd1_set", "shift1_set",
                             "x1_set"))
        x1t_mm, x1t_hi_set, x1t_lo_set = (sem(n) for n in ("x1t_mm", "x1t_hi_set", "x1t_lo_set"))
        g_mm, g_hi_set, g_lo_set, x1_bv_set = (
            sem(n) for n in ("g_mm", "g_hi_set", "g_lo_set", "x1_bv_set"))
        vs_mm, vs_read, v_lo_set, w_set, wt_hi_set, wt_lo_set = (
            sem(n) for n in ("vs_mm", "vs_read", "v_lo_set", "w_set", "wt_hi_set", "wt_lo_set"))
        o_mm, den_set, den_inv_set, o_scale_set, y2_set = (
            sem(n) for n in ("o_mm", "den_set", "den_inv_set", "o_scale_set", "y2_set"))
        stats2_set, mean2_set, var2_set, rstd2_set, shift2_set, y_out_set = (
            sem(n) for n in ("stats2_set", "mean2_set", "var2_set", "rstd2_set", "shift2_set", "y_out_set"))

        by_chunk = "(c p) n -> p c n"
        block = ctx.enter_context(nc.Block())

        @block.sync
        def _(sp):
            def load(q):
                if q.has(4):
                    sp.wait_ge(xt_lo_set, q.count(1, -3))
                sp.dma_start(xt_in[:, q.slot(4)], xt[q.index()]).then_inc(xt_loaded[q.slot(4)], 16)
                if q.has(4):
                    sp.wait_ge(y1_set, q.count(1, -3))
                sp.dma_start(x_in[:, q.slot(4)], x[q.index()]).then_inc(x_loaded[q.slot(4)], 16)
                if q.has(4):
                    sp.wait_ge(w_set, q.count(1, -3))
                sp.dma_start(adjt_in[:, q.slot(4)], adjt[q.index()]).then_inc(adjt_loaded[q.slot(4)], 16)

            def store(q):
                sp.wait_ge(y_out_set, q.count(1, 1))
                sp.dma_start(out[q.index()], y_out[:, q.slot(2)]).then_inc(stored[q.slot(2)], 16)

            for n in range(UNROLL + 1):
                load(Pair(0, n))
            with sp.Fori(0, PAIRS - UNROLL - 4, UNROLL) as i:
                for k in range(UNROLL):
                    load(Pair(i, k + UNROLL + 1))
                    store(Pair(i, k))
            for n in range(PAIRS - UNROLL - 4, PAIRS):
                if n + UNROLL + 1 < PAIRS:
                    load(Pair(0, n + UNROLL + 1))
                store(Pair(0, n))
            for n in range(2):
                sp.wait_ge(stored[n], 16 * (PAIRS // 2 + 1))

        @block.gpsimd
        def _(pool):
            nc.gpsimd.memset(bias_raw[:], 0.0).then_inc(bias_zero, 1)
            nc.gpsimd.memset(ident[:], 0.0).then_inc(ident_set, 1)
            nc.gpsimd.memset(ones_col[:], 1.0).then_inc(consts_set, 1)
            nc.gpsimd.memset(ones_bf[:], 1.0).then_inc(consts_set, 1)
            nc.gpsimd.memset(minus_half[:], -0.5).then_inc(consts_set, 1)
            pool.wait_ge(ident_set, 1)
            nc.gpsimd.affine_select(out=ident[:], in_=ident[:], compare_op=ALU.not_equal, fill=1.0, base=0,
                                    pattern=[[-1, 128]], channel_multiplier=1).then_inc(ident_set, 1)
            pool.wait_ge(consts_set, 3)
            pool.wait_ge(ld_v, 32)

            def step(q):
                q0, q1, q2, q3, q4 = q
                if q3.exists():
                    pool.wait_ge(x1_set, q3.count(1, 1))
                    for g in range(PG):
                        last = nc.gpsimd.tensor_tensor(x1_bv[:, q3.slot(2), g], x1[:, g], bv_all[:], ALU.add)
                    last.then_inc(x1_bv_set, 1)
                if q0.exists():
                    pool.wait_ge(xt_hi_set, q0.count(1, 1))
                    nc.gpsimd.tensor_tensor(xt_lo[:, q0.slot(4)], xt_in[:, q0.slot(4)],
                                            xt_hi[:, q0.slot(4)].bitcast(F32), ALU.subtract).then_inc(xt_lo_set, 1)
                if q1.exists():
                    pool.wait_ge(adjt_loaded[q1.slot(4)], q1.turns(4, 1))
                    pool.wait_ge(e_max_set, q1.count(1, 1))
                    nc.gpsimd.tensor_tensor(alpha[:], adjt_in[:, q1.slot(4)], e_max[:], ALU.mult).then_inc(alpha_set, 1)
                if q4.exists():
                    pool.wait_ge(var2_set, q4.count(1, 1))
                    nc.gpsimd.tensor_tensor(rstd2[:], var_eps2[:], minus_half[:], ALU.pow).then_inc(rstd2_set, 1)
                    pool.wait_ge(rstd2_set, q4.count(1, 1))
                    nc.gpsimd.tensor_tensor(shift2[:], minus_mean2[:], rstd2[:], ALU.mult).then_inc(shift2_set, 1)
                if q2.exists():
                    pool.wait_ge(var1_set, q2.count(1, 1))
                    nc.gpsimd.tensor_tensor(rstd1[:], var_eps1[:], minus_half[:], ALU.pow).then_inc(rstd1_set, 1)
                    pool.wait_ge(rstd1_set, q2.count(1, 1))
                    nc.gpsimd.tensor_tensor(shift1[:], minus_mean1[:], rstd1[:], ALU.mult).then_inc(shift1_set, 1)
                if q3.exists():
                    pool.wait_ge(vs_read, q3.count(2, 2))
                    nc.gpsimd.tensor_tensor(w_all[:], adjt_in[:, q3.slot(4)], e_score[:], ALU.mult).then_inc(w_set, 1)
                    pool.wait_ge(wt_hi_set, q3.count(1, 1))
                    nc.gpsimd.tensor_tensor(wt_lo[:], w_all[:], wt_hi[:].bitcast(F32), ALU.subtract).then_inc(wt_lo_set, 1)

            run_steps(pool, step)

        @block.scalar
        def _(act):
            act.dma_start(cols[:], columns).then_inc(ld_cols, 16)
            act.dma_start(wv0t_raw[:], Wv0t.rearrange(by_chunk, p=128)).then_inc(ld_cols, 16)
            act.dma_start(ab_all[:], ab.partition_broadcast(128)).then_inc(ld_cols, 16)
            for n in range(3):
                act.dma_start(w_raw[:, :, n * D:(n + 1) * D], Wk0[n].rearrange(by_chunk, p=128)).then_inc(ld_w, 16)
            act.wait_ge(bias_zero, 1)
            for r in (0, 32, 64):
                act.dma_start(bias_raw[r:r + 3, :], bk0).then_inc(ld_bias, 16)
            act.dma_start(wq1_raw[:], Wq1.rearrange(by_chunk, p=128)).then_inc(ld_m, 16)
            act.dma_start(wk1_raw[:], Wk1.rearrange(by_chunk, p=128)).then_inc(ld_m, 16)
            act.dma_start(v_raw[:, :, 0:D], Wv1t.rearrange(by_chunk, p=128)).then_inc(ld_v, 16)
            act.dma_start(bv_all[:], bv1.partition_broadcast(128)).then_inc(ld_v, 16)

            act.wait_ge(ld_w, 48)
            act.wait_ge(setup_cols, 2)
            nc.scalar.copy(w_hi[:], w_raw[:]).then_inc(setup_hi, 1)
            act.wait_ge(setup_mm, 2)
            nc.scalar.copy(m_hi[:], u[:]).then_inc(setup_hi, 1)
            act.wait_ge(setup_cols, 4)
            for g in range(PG):
                nc.scalar.copy(gv_hi[:, g, :, 0:V_COLS], v_raw[:]).then_inc(setup_hi, 1)

            def step(q):
                q0, q1, q2, q3, q4 = q
                if q3.exists():
                    act.wait_ge(x1t_mm, q3.count(1, 1))
                    nc.scalar.copy(x1t_hi[:], xg[:]).then_inc(x1t_hi_set, 1)
                if q1.exists():
                    for g in range(PG):
                        act.wait_ge(z_mm, q1.count(2, 1 + g))
                        nc.scalar.copy(z_hi[:, g], z[:, g, 0:D]).then_inc(z_hi_set, 1)
                if q2.exists():
                    act.wait_ge(u_mm, q2.count(1, 1))
                    nc.scalar.copy(u_hi[:], u[:]).then_inc(u_hi_set, 1)
                if q0.exists():
                    act.wait_ge(xt_loaded[q0.slot(4)], q0.turns(4, 1))
                    nc.scalar.copy(xt_hi[:, q0.slot(4)], xt_in[:, q0.slot(4)]).then_inc(xt_hi_set, 1)
                if q3.exists():
                    act.wait_ge(g_mm, q3.count(1, 1))
                    for c in range(C):
                        last = nc.scalar.activation(gv_hi[:, :, c, V_COLS:], xg[:, c], ACT.Identity,
                                                    bias=u_col[:, c:c + 1])
                    last.then_inc(g_hi_set, 1)
                if q1.exists():
                    act.wait_ge(s_spread_mm, q1.count(1, 1))
                    for g in range(PG):
                        nc.scalar.activation(e_full[:, g], spread_n[:, g], ACT.Exp, bias=s_cols[:, g, 0:1])
                        last = nc.scalar.activation(e_slope[:, g], spread_n[:, g], ACT.Exp,
                                                    bias=s_cols[:, g, 2:3], scale=SLOPE)
                    last.then_inc(e_set, 1)

                def read_vs(g):
                    act.wait_ge(vs_mm, q3.count(2, 1 + g))
                    nc.scalar.activation(e_score[:, g], vo[:, g, V_COLS:VS_COLS], ACT.Exp)
                    nc.scalar.activation(e_c[:, g:g + 1], vo[:, g, D:D + 1], ACT.Exp, bias=c_const[:])
                    nc.scalar.copy(v_hi[:, g, 0:D], vo[:, g, 0:D]).then_inc(vs_read, 1)

                if q3.exists():
                    read_vs(0)
                if q4.exists():
                    act.wait_ge(stored[q4.slot(2)], q4.turns(2, 1))
                    act.wait_ge(shift2_set, q4.count(1, 1))
                    for g in range(PG):
                        last = nc.scalar.activation(y_out[:, q4.slot(2), g], y2[:, g], ACT.Identity,
                                                    bias=shift2[:, g:g + 1], scale=rstd2[:, g:g + 1])
                    last.then_inc(y_out_set, 1)
                if q3.exists():
                    read_vs(1)
                if q1.exists():
                    act.wait_ge(t_set, q1.count(1, 1))
                    nc.scalar.copy(t_hi[:], t_all[:]).then_inc(t_hi_set, 1)
                if q2.exists():
                    act.wait_ge(shift1_set, q2.count(1, 1))
                    for g in range(PG):
                        last = nc.scalar.activation(x1[:, g], y1[:, g], ACT.Identity,
                                                    bias=shift1[:, g:g + 1], scale=rstd1[:, g:g + 1])
                    last.then_inc(x1_set, 1)
                if q3.exists():
                    act.wait_ge(w_set, q3.count(1, 1))
                    nc.scalar.copy(wt_hi[:], w_all[:]).then_inc(wt_hi_set, 1)

            act.wait_ge(setup_lo, 1)
            run_steps(act, step)

        @block.vector
        def _(dve):
            nc.vector.memset(w_raw[:, :, W_COLS - 1:W_COLS], 0.0).then_inc(stored[0], 16)
            nc.vector.memset(v_raw[:, :, V_COLS - 1:V_COLS], 0.0).then_inc(stored[1], 16)
            nc.vector.memset(v_hi[:, :, D:D + 1].bitcast(F32), 1.0)
            nc.vector.memset(v_hi[:, :, D + 1:D + 2].bitcast(F32), 0.0)
            nc.vector.memset(v_lo[:, :, D:D + 2].bitcast(F32), 0.0)
            nc.vector.memset(s_const[:, 3:4], 0.0).then_inc(setup_cols, 1)

            dve.wait_ge(setup_mm, 1)
            wji = small[:, 0:2 * C].rearrange("p (c n) -> p c n", n=2)
            nc.vector.tensor_copy(w_raw[:, :, 3 * D:3 * D + 2], wji)
            nc.vector.tensor_scalar(w_raw[:, :, 3 * D + 2:3 * D + 3], wji[:, :, 0:1], SLOPE, None,
                                    ALU.mult).then_inc(setup_cols, 1)
            dve.wait_ge(ld_cols, 48)
            nc.vector.tensor_scalar(s_const[:, 0:1], small[:, 8:9], ab_all[:], None, ALU.add)
            nc.vector.tensor_scalar(s_const[:, 2:3], small[:, 8:9], ab_all[:], SLOPE, ALU.add, ALU.mult)
            nc.vector.tensor_copy(s_const[:, 1:2], small[:, 9:10])
            dve.wait_ge(setup_mm, 3)
            nc.vector.tensor_copy(u_col[:], small1[:, 16:16 + C])
            nc.vector.tensor_copy(c_const[:], small1[:, 24:25]).then_inc(setup_cols, 1)
            dve.wait_ge(ld_v, 32)
            nc.vector.tensor_copy(v_raw[:, :, D:D + 1],
                                  small1[:, 20:20 + C].rearrange("p (c n) -> p c n", n=1)).then_inc(setup_cols, 1)
            dve.wait_ge(setup_hi, 1)
            nc.vector.tensor_tensor(w_lo[:], w_raw[:], w_hi[:].bitcast(F32), ALU.subtract).then_inc(setup_lo, 1)
            dve.wait_ge(setup_hi, 2)
            nc.vector.tensor_tensor(m_lo[:], u[:], m_hi[:].bitcast(F32), ALU.subtract).then_inc(setup_lo, 1)
            dve.wait_ge(setup_hi, 2 + PG)
            for g in range(PG):
                nc.vector.tensor_tensor(gv_lo[:, g, :, 0:V_COLS], v_raw[:], gv_hi[:, g, :, 0:V_COLS].bitcast(F32),
                                        ALU.subtract).then_inc(setup_lo, 1)
            dve.wait_ge(ld_bias, 48)
            nc.vector.tensor_copy(bias_hi[:], bias_raw[:]).then_inc(bias_split, 1)
            dve.wait_ge(bias_split, 1)
            nc.vector.tensor_tensor(bias_rest[:], bias_raw[:], bias_hi[:], ALU.subtract).then_inc(bias_split, 1)
            dve.wait_ge(bias_split, 2)
            nc.vector.tensor_copy(bias_mid[:], bias_rest[:]).then_inc(bias_split, 1)
            dve.wait_ge(bias_split, 3)
            nc.vector.tensor_tensor(bias_low[:], bias_rest[:], bias_mid[:], ALU.subtract).then_inc(bias_split, 1)
            dve.wait_ge(bias_split, 4)
            nc.vector.tensor_copy(bias_parts[0:32], bias_hi[0:32]).then_inc(bias_split, 1)
            nc.vector.tensor_copy(bias_parts[32:64], bias_mid[32:64]).then_inc(bias_split, 1)
            nc.vector.tensor_copy(bias_parts[64:128], bias_low[64:128]).then_inc(bias_split, 1)

            def step(q):
                q0, q1, q2, q3, q4 = q
                if q3.exists():
                    dve.wait_ge(x1t_hi_set, q3.count(1, 1))
                    nc.vector.tensor_tensor(x1t_lo[:], xg[:], x1t_hi[:].bitcast(F32), ALU.subtract).then_inc(x1t_lo_set, 1)
                if q1.exists():
                    for g in range(PG):
                        dve.wait_ge(z_hi_set, q1.count(2, 1 + g))
                        nc.vector.tensor_tensor(s_cols[:, g], z[:, g, D:Z_COLS], s_const[:], ALU.add)
                        nc.vector.tensor_tensor(z_lo[:, g], z[:, g, 0:D], z_hi[:, g].bitcast(F32),
                                                ALU.subtract).then_inc(z_lo_set, 1)
                if q4.exists():
                    dve.wait_ge(o_mm, q4.count(1, 1))
                    nc.vector.tensor_tensor(den[:], vo[:, :, D], e_c[:], ALU.mult).then_inc(den_set, 1)
                if q2.exists():
                    dve.wait_ge(u_hi_set, q2.count(1, 1))
                    nc.vector.tensor_tensor(u_lo[:], u[:], u_hi[:].bitcast(F32), ALU.subtract).then_inc(u_lo_set, 1)
                if q4.exists():
                    dve.wait_ge(den_set, q4.count(1, 1))
                    nc.vector.reciprocal(den_inv[:], den[:]).then_inc(den_inv_set, 1)
                    dve.wait_ge(den_inv_set, q4.count(1, 1))
                    nc.vector.tensor_tensor(o_scale[:], den_inv[:], e_c[:], ALU.mult).then_inc(o_scale_set, 1)
                    dve.wait_ge(x1_bv_set, q4.count(1, 1))
                    dve.wait_ge(o_scale_set, q4.count(1, 1))
                    for g in range(PG):
                        last = nc.vector.scalar_tensor_tensor(
                            out=y2[:, g], in0=vo[:, g, 0:D], scalar=o_scale[:, g:g + 1],
                            in1=x1_bv[:, q4.slot(2), g], op0=ALU.mult, op1=ALU.add)
                    last.then_inc(y2_set, 1)
                if q3.exists():
                    dve.wait_ge(g_hi_set, q3.count(1, 1))
                    for c in range(C):
                        last = nc.vector.scalar_tensor_tensor(
                            out=gv_lo[:, :, c, V_COLS:], in0=xg[:, c], scalar=u_col[:, c:c + 1],
                            in1=gv_hi[:, :, c, V_COLS:].bitcast(F32), op0=ALU.add, op1=ALU.subtract)
                    last.then_inc(g_lo_set, 1)
                if q4.exists():
                    dve.wait_ge(y2_set, q4.count(1, 1))
                    for g in range(PG):
                        last = nc.vector.bn_stats(stats2[:, g], y2[:, g])
                    last.then_inc(stats2_set, 1)
                    dve.wait_ge(stats2_set, q4.count(1, 1))
                if q1.exists():
                    dve.wait_ge(e_set, q1.count(1, 1))
                    nc.vector.tensor_tensor(e_max[:], e_full[:], e_slope[:], ALU.max).then_inc(e_max_set, 1)
                if q4.exists():
                    for g in range(PG):
                        last = nc.vector.bn_aggr(mean_var2[:, g], stats2[:, g])
                    last.then_inc(mean2_set, 1)
                    dve.wait_ge(mean2_set, q4.count(1, 1))
                    nc.vector.tensor_scalar(minus_mean2[:], mean_var2[:, :, 0], -1.0, None, ALU.mult)
                    nc.vector.tensor_scalar(var_eps2[:], mean_var2[:, :, 1], LN_EPS, None, ALU.add).then_inc(var2_set, 1)
                if q2.exists():
                    dve.wait_ge(x_loaded[q2.slot(4)], q2.turns(4, 1))
                    dve.wait_ge(h_mm, q2.count(1, 1))
                    nc.vector.scalar_tensor_tensor(out=y1[:], in0=h[:], scalar=0.0, in1=x_in[:, q2.slot(4)],
                                                   op0=ALU.max, op1=ALU.add).then_inc(y1_set, 1)
                    dve.wait_ge(y1_set, q2.count(1, 1))
                    for g in range(PG):
                        last = nc.vector.bn_stats(stats1[:, g], y1[:, g])
                    last.then_inc(stats1_set, 1)
                    dve.wait_ge(stats1_set, q2.count(1, 1))
                if q1.exists():
                    dve.wait_ge(row_sum_mm, q1.count(1, 1))
                    nc.vector.tensor_scalar(row_sum_eps[:], row_sum, ROW_EPS, None, ALU.add).then_inc(row_sum_set, 1)
                if q2.exists():
                    for g in range(PG):
                        last = nc.vector.bn_aggr(mean_var1[:, g], stats1[:, g])
                    last.then_inc(mean1_set, 1)
                if q1.exists():
                    dve.wait_ge(row_sum_set, q1.count(1, 1))
                    nc.vector.reciprocal(row_inv[:], row_sum_eps[:]).then_inc(row_inv_set, 1)
                if q2.exists():
                    dve.wait_ge(mean1_set, q2.count(1, 1))
                    nc.vector.tensor_scalar(minus_mean1[:], mean_var1[:, :, 0], -1.0, None, ALU.mult)
                    nc.vector.tensor_scalar(var_eps1[:], mean_var1[:, :, 1], LN_EPS, None, ALU.add).then_inc(var1_set, 1)

                def low_v(g):
                    dve.wait_ge(vs_read, q3.count(2, 1 + g))
                    nc.vector.tensor_tensor(v_lo[:, g, 0:D], vo[:, g, 0:D], v_hi[:, g, 0:D].bitcast(F32),
                                            ALU.subtract).then_inc(v_lo_set, 1)

                if q3.exists():
                    low_v(0)
                if q1.exists():
                    dve.wait_ge(inv_spread_mm, q1.count(1, 1))
                    nc.vector.tensor_tensor(t_all[:], alpha[:], spread_n, ALU.mult).then_inc(t_set, 1)
                if q3.exists():
                    low_v(1)
                if q1.exists():
                    dve.wait_ge(t_hi_set, q1.count(1, 1))
                    nc.vector.tensor_tensor(t_lo[:], t_all[:], t_hi[:].bitcast(F32), ALU.subtract).then_inc(t_lo_set, 1)

            run_steps(dve, step)

        @block.tensor
        def _(pe):
            mm = nc.tensor.matmul

            def split_product(to, stationary, moving, start, stop):
                terms = [(s[i], m[j]) for s, m in zip(stationary, moving) for i, j in ((0, 0), (0, 1), (1, 0))]
                for n, (s, m) in enumerate(terms):
                    last = mm(to, s, m, start=start and n == 0, stop=stop and n == len(terms) - 1,
                              skip_group_check=True)
                return last

            pe.wait_ge(ld_cols, 48)
            for c in range(C):
                for o in range(C):
                    last = mm(small[:, 2 * c:2 * c + 2], wv0t_raw[:, o, c * 128:(c + 1) * 128], cols[:, o, 0:2],
                              start=(o == 0), stop=(o == C - 1))
            for o in range(C):
                last = mm(small[:, 8:10], cols[:, o, 2:3].to_broadcast([128, 128]), cols[:, o, 0:2],
                          start=(o == 0), stop=(o == C - 1))
            last.then_inc(setup_mm, 1)
            pe.wait_ge(ld_m, 32)
            for c in range(C):
                for o in range(C):
                    last = mm(u[:, c], wq1_raw[:, o, c * 128:(c + 1) * 128], wk1_raw[:, o, :],
                              start=(o == 0), stop=(o == C - 1))
            last.then_inc(setup_mm, 1)
            for c in range(C):
                for o in range(C):
                    mm(small1[:, 16 + c:17 + c], wk1_raw[:, o, c * 128:(c + 1) * 128], cols[:, o, 3:4],
                       start=(o == 0), stop=(o == C - 1))
                for o in range(C):
                    mm(small1[:, 20 + c:21 + c], wq1_raw[:, o, c * 128:(c + 1) * 128], cols[:, o, 4:5],
                       start=(o == 0), stop=(o == C - 1))
            for o in range(C):
                last = mm(small1[:, 24:25], cols[:, o, 3:4].to_broadcast([128, 128]), cols[:, o, 4:5],
                          start=(o == 0), stop=(o == C - 1))
            last.then_inc(setup_mm, 1)
            pe.wait_ge(ident_set, 2)
            pe.wait_ge(consts_set, 3)
            pe.wait_ge(bias_split, 7)
            pe.wait_ge(setup_lo, 2 + PG)

            def weights(lo, hi):
                return [(w_hi[:, c, lo:hi], w_lo[:, c, lo:hi]) for c in range(C)]

            def xt_of(q, g):
                return [(xt_hi[:, q.slot(4), c, g], xt_lo[:, q.slot(4), c, g]) for c in range(C)]

            def step(q):
                q0, q1, q2, q3, q4 = q
                if q1.exists():
                    pe.wait_ge(xt_lo_set, q1.count(1, 1))
                    for g in range(PG):
                        split_product(z[:, g, 0:Z_COLS], xt_of(q1, g), weights(2 * D, W_COLS), True,
                                      True).then_inc(z_mm, 1)
                if q4.exists():
                    pe.wait_ge(wt_lo_set, q4.count(1, 1))
                    pe.wait_ge(v_lo_set, q4.count(2, 2))
                    for g in range(PG):
                        last = split_product(vo[:, g, 0:V_COLS], [(wt_hi[:, g], wt_lo[:, g])],
                                             [(v_hi[:, g], v_lo[:, g])], True, True)
                    last.then_inc(o_mm, 1)
                if q3.exists():
                    pe.wait_ge(x1t_lo_set, q3.count(1, 1))
                    for c in range(C):
                        last = split_product(
                            xg[:, c], [(m_hi[:, k, c * 128:(c + 1) * 128], m_lo[:, k, c * 128:(c + 1) * 128])
                                       for k in range(C)],
                            [(x1t_hi[:, k], x1t_lo[:, k]) for k in range(C)], True, True)
                    last.then_inc(g_mm, 1)
                if q1.exists():
                    pe.wait_ge(z_lo_set, q1.count(2, 2))
                    for g in range(PG):
                        last = nc.tensor.transpose(spread_n[:, g], s_cols[:, g, 1:2].to_broadcast([128, N]), ident[:])
                    last.then_inc(s_spread_mm, 1)
                if q2.exists():
                    wait(pe, y1_set, q2.count(1, 0))
                    for g in range(PG):
                        mm(h[:, g], ones_bf[:], bias_parts[:], start=g == 0, stop=False, skip_group_check=True)
                        split_product(h[:, g], xt_of(q2, g), weights(0, D), False, False)
                    pe.wait_ge(u_lo_set, q2.count(1, 1))
                    for g in range(PG):
                        last = split_product(h[:, g], [(t_hi[:, g], t_lo[:, g])], [(u_hi[:, g], u_lo[:, g])],
                                             False, g == PG - 1)
                    last.then_inc(h_mm, 1)

                def values_and_scores(g):
                    split_product(vo[:, g, 0:VS_COLS], [(x1t_hi[:, c, g], x1t_lo[:, c, g]) for c in range(C)],
                                  [(gv_hi[:, g, c], gv_lo[:, g, c]) for c in range(C)], True, True).then_inc(vs_mm, 1)

                if q3.exists():
                    pe.wait_ge(g_lo_set, q3.count(1, 1))
                    wait(pe, y2_set, q3.count(1, 0))
                    values_and_scores(0)
                if q1.exists():
                    pe.wait_ge(alpha_set, q1.count(1, 1))
                    for g in range(PG):
                        last = mm(row_sum[:, g:g + 1], alpha[:, g], ones_col[:], start=True, stop=True)
                    last.then_inc(row_sum_mm, 1)
                if q3.exists():
                    values_and_scores(1)
                if q1.exists():
                    pe.wait_ge(row_inv_set, q1.count(1, 1))
                    for g in range(PG):
                        last = nc.tensor.transpose(spread_n[:, g], row_inv[:, g:g + 1].to_broadcast([128, N]), ident[:])
                    last.then_inc(inv_spread_mm, 1)
                    for g in range(PG):
                        split_product(u[:, g], xt_of(q1, g), weights(D, 2 * D), g == 0, False)
                    pe.wait_ge(t_lo_set, q1.count(1, 1))
                    for g in range(PG):
                        last = split_product(u[:, g], [(t_hi[:, g], t_lo[:, g])], [(z_hi[:, g], z_lo[:, g])],
                                             False, g == PG - 1)
                    last.then_inc(u_mm, 1)
                if q2.exists():
                    pe.wait_ge(x1_set, q2.count(1, 1))
                    for g in range(PG):
                        for c in range(C):
                            last = nc.tensor.transpose(xg[:, c, g], x1[:, g, c * 128:(c + 1) * 128], ident[:])
                    last.then_inc(x1t_mm, 1)

            run_steps(pe, step)


def kernel(**inputs):
    import numpy as np
    import concourse.bacc as bacc
    from concourse.bass_utils import run_bass_kernel_spmd

    a = {k: np.asarray(v) for k, v in inputs.items()}
    x, adj = a["x"], a["adj"]
    aw = a["L0_gnn_aw"][:, 0]
    columns = np.stack([aw[:D], aw[D:], a["L0_gnn_bv"], a["L1_gnn_Wq_b"], a["L1_gnn_Wk_b"]], axis=-1)
    arrays = {
        "x": x.reshape(PAIRS, PG, N, D).transpose(0, 2, 1, 3),
        "xt": x.reshape(PAIRS, PG, N, C, 128).transpose(0, 4, 3, 1, 2),
        "adjt": adj.reshape(PAIRS, PG, N, N).transpose(0, 3, 1, 2),
        "columns": columns.reshape(C, 128, 5).transpose(1, 0, 2),
        "Wv0t": a["L0_gnn_Wv"].T,
        "ab": a["L0_gnn_ab"],
        "Wk0": a["L0_gnn_Wk"],
        "bk0": a["L0_gnn_bk"],
        "Wq1": a["L1_gnn_Wq_w"],
        "Wk1": a["L1_gnn_Wk_w"],
        "Wv1t": a["L1_gnn_Wv_w"].T,
        "bv1": a["L1_gnn_Wv_b"],
    }
    nc = bacc.Bacc("TRN2", target_bir_lowering=False, num_devices=1)
    feed, args = {}, []
    for name, value in arrays.items():
        value = np.ascontiguousarray(value)
        feed[f"in_{name}"] = value
        args.append(nc.dram_tensor(f"in_{name}", value.shape, F32, kind="ExternalInput").ap())
    args.append(nc.dram_tensor("out", (PAIRS, N, PG, D), F32, kind="ExternalOutput").ap())
    two_layer_graph_kernel(nc, *args)
    result = run_bass_kernel_spmd(nc, [feed], core_ids=[0]).results[0]["out"]
    return np.ascontiguousarray(result.transpose(0, 2, 1, 3).reshape(B, N, D))
```

```python
from contextlib import ExitStack

import concourse.bass as bass
from concourse import mybir

F32 = mybir.dt.float32
F32R = mybir.dt.float32r
BF16 = mybir.dt.bfloat16
ALU = mybir.AluOpType
ACT = mybir.ActivationFunctionType

B, N, D = 64, 128, 256
PG = 2
PAIRS = B // PG
C = D // 128
SLOPE = 0.2
ROW_EPS = 1e-12
LN_EPS = 1e-5
UNROLL = 4
LAGS = 4
AHEAD = 5
W_COLS = 3 * D + 4
Z_COLS = D + 4
V_COLS = D + 2
VS_COLS = V_COLS + N


class Pair:

    def __init__(self, base, shift):
        self.base, self.shift = base, shift

    def exists(self):
        return not isinstance(self.base, int) or 0 <= self.base + self.shift < PAIRS

    def slot(self, ring):
        return (self.base + self.shift if isinstance(self.base, int) else self.shift) % ring

    def index(self):
        return self.base + self.shift

    def is_first(self):
        return isinstance(self.base, int) and self.base + self.shift == 0

    def count(self, per_pair, extra):
        if isinstance(self.base, int):
            return per_pair * (self.base + self.shift) + extra
        return self.base * per_pair + (per_pair * self.shift + extra)

    def turns(self, ring, extra):
        if isinstance(self.base, int):
            return 16 * ((self.base + self.shift) // ring + extra)
        return self.base * (16 // ring) + 16 * (self.shift // ring + extra)

    def has(self, before):
        return not isinstance(self.base, int) or self.base + self.shift - before >= 0


def run_steps(engine, step):
    for p in range(UNROLL):
        step([Pair(0, p - lag) for lag in range(LAGS + 1)])
    with engine.Fori(UNROLL, PAIRS, UNROLL) as i:
        for k in range(UNROLL):
            step([Pair(i, k - lag) for lag in range(LAGS + 1)])
    for p in range(PAIRS, PAIRS + LAGS):
        step([Pair(0, p - lag) for lag in range(LAGS + 1)])


def wait(engine, sem, value):
    if not isinstance(value, int) or value > 0:
        engine.wait_ge(sem, value)


def two_layer_graph_kernel(nc, x, xt, adjt, columns, Wv0t, ab, Wk0, bk0, Wq1, Wk1, Wv1t, bv1, out):
    with ExitStack() as ctx:
        def sb(name, shape, dt=F32):
            return ctx.enter_context(nc.sbuf_tensor(name, shape, dt))

        def psum(name, shape):
            return ctx.enter_context(nc.psum_tensor(name, shape, F32))

        def sem(name):
            return ctx.enter_context(nc.semaphore(name))

        w_raw = sb("w_raw", [128, C, W_COLS])
        w_hi, w_lo = (sb(n, [128, C, W_COLS], F32R) for n in ("w_hi", "w_lo"))
        wv0t_raw = sb("wv0t_raw", [128, C, D])
        wq1_raw = sb("wq1_raw", [128, C, D])
        wk1_raw = sb("wk1_raw", [128, C, D + 1])
        v_raw = sb("v_raw", [128, C, V_COLS])
        m_hi, m_lo = (sb(n, [128, C, D], F32R) for n in ("m_hi", "m_lo"))
        cols = sb("cols", [128, C, 5])
        ab_all = sb("ab_all", [128, 1])
        s_const = sb("s_const", [128, 4])
        u_col = sb("u_col", [128, C])
        c_const = sb("c_const", [128, 1])
        bv_all = sb("bv_all", [128, D])
        bias_raw = sb("bias_raw", [128, D])
        bias_rest = sb("bias_rest", [128, D])
        bias_hi, bias_mid, bias_low, bias_parts = (
            sb(n, [128, D], BF16) for n in ("bias_hi", "bias_mid", "bias_low", "bias_parts"))
        ones_bf = sb("ones_bf", [128, 128], BF16)
        ones_col = sb("ones_col", [128, 1])
        ident = sb("ident", [128, 128])
        minus_half = sb("minus_half", [128, PG])

        xt_in = sb("xt_in", [128, 4, C, PG, N])
        x_in = sb("x_in", [128, 4, PG, D])
        adjt_in = sb("adjt_in", [128, 4, PG, N])
        y_out = sb("y_out", [128, 2, PG, D])
        xt_hi, xt_lo = (sb(n, [128, 4, C, PG, N], F32R) for n in ("xt_hi", "xt_lo"))
        s_cols = sb("s_cols", [128, PG, 4])
        z_hi, z_lo = (sb(n, [128, 2, PG, D], F32R) for n in ("z_hi", "z_lo"))
        e_full, e_slope, e_max, alpha, t_all = (
            sb(n, [128, PG, N]) for n in ("e_full", "e_slope", "e_max", "alpha", "t_all"))
        row_sum_eps, row_inv = (sb(n, [128, PG]) for n in ("row_sum_eps", "row_inv"))
        t_hi, t_lo = (sb(n, [128, PG, N], F32R) for n in ("t_hi", "t_lo"))
        u_hi, u_lo = (sb(n, [128, PG, D], F32R) for n in ("u_hi", "u_lo"))
        y1 = sb("y1", [128, PG, D])
        stats1 = sb("stats1", [128, PG, 6])
        mean_var1 = sb("mean_var1", [128, PG, 2])
        var_eps1, minus_mean1, rstd1, shift1 = (
            sb(n, [128, PG]) for n in ("var_eps1", "minus_mean1", "rstd1", "shift1"))
        x1 = sb("x1", [128, PG, D])
        x1t_hi, x1t_lo = (sb(n, [128, C, PG, N], F32R) for n in ("x1t_hi", "x1t_lo"))
        gv_hi, gv_lo = (sb(n, [128, PG, C, VS_COLS], F32R) for n in ("gv_hi", "gv_lo"))
        x1_bv = sb("x1_bv", [128, 2, PG, D])
        e_score, w_all = (sb(n, [128, PG, N]) for n in ("e_score", "w_all"))
        wt_hi, wt_lo = (sb(n, [128, PG, N], F32R) for n in ("wt_hi", "wt_lo"))
        v_hi, v_lo = (sb(n, [128, PG, V_COLS], F32R) for n in ("v_hi", "v_lo"))
        e_c, den, den_inv, o_scale = (sb(n, [128, PG]) for n in ("e_c", "den", "den_inv", "o_scale"))
        y2 = sb("y2", [128, PG, D])
        stats2 = sb("stats2", [128, PG, 6])
        mean_var2 = sb("mean_var2", [128, PG, 2])
        var_eps2, minus_mean2, rstd2, shift2 = (
            sb(n, [128, PG]) for n in ("var_eps2", "minus_mean2", "rstd2", "shift2"))

        z = psum("z", [128, PG, 2 * D])
        spread = psum("spread", [128, 2 * D])
        u = psum("u", [128, PG, D])
        h = psum("h", [128, PG, D])
        xg = psum("xg", [128, C, PG, N])
        vo = psum("vo", [128, PG, 2 * D])
        spread_n = spread[:, 0:PG * N].rearrange("p (g n) -> p g n", g=PG)
        row_sum = spread[:, PG * N:PG * N + PG]
        s_setup, m_setup, u_setup = xg[:, 0, 0], vo[:, :, 0:D + 1], xg[:, 0, 1]

        ld_w = [sem(f"ld_w{n}") for n in range(3)]
        ld_cols, ld_wv0t, ld_ab, ld_m, ld_v, ld_bias = (
            sem(n) for n in ("ld_cols", "ld_wv0t", "ld_ab", "ld_m", "ld_v", "ld_bias"))
        consts_set, bias_zero, ident_set = (sem(n) for n in ("consts_set", "bias_zero", "ident_set"))
        s_setup_mm, m_setup_mm, s_cols_ready, bk_ready, s_const_set, m_cols_ready = (
            sem(n) for n in ("s_setup_mm", "m_setup_mm", "s_cols_ready", "bk_ready", "s_const_set",
                             "m_cols_ready"))
        w_hi_set, w_lo_set, m_hi_set, m_lo_set, bias_split = (
            sem(n) for n in ("w_hi_set", "w_lo_set", "m_hi_set", "m_lo_set", "bias_split"))
        xt_loaded = [sem(f"xt_loaded{n}") for n in range(4)]
        x_loaded = [sem(f"x_loaded{n}") for n in range(4)]
        adjt_loaded = [sem(f"adjt_loaded{n}") for n in range(4)]
        stored = [sem(f"stored{n}") for n in range(2)]
        xt_hi_set, xt_lo_set = sem("xt_hi_set"), sem("xt_lo_set")
        z_mm, z_hi_set, z_lo_set = sem("z_mm"), sem("z_hi_set"), sem("z_lo_set")
        s_spread_mm, e_set, e_max_set, alpha_set = (
            sem(n) for n in ("s_spread_mm", "e_set", "e_max_set", "alpha_set"))
        row_sum_mm, row_sum_set, row_inv_set, inv_spread_mm, t_set, t_hi_set, t_lo_set = (
            sem(n) for n in ("row_sum_mm", "row_sum_set", "row_inv_set", "inv_spread_mm", "t_set",
                             "t_hi_set", "t_lo_set"))
        u_mm, u_hi_set, u_lo_set, h_mm = (sem(n) for n in ("u_mm", "u_hi_set", "u_lo_set", "h_mm"))
        y1_set, stats1_set, mean1_set, var1_set, rstd1_set, shift1_set, x1_set = (
            sem(n) for n in ("y1_set", "stats1_set", "mean1_set", "var1_set", "rstd1_set", "shift1_set",
                             "x1_set"))
        x1t_mm, x1t_hi_set, x1t_lo_set = (sem(n) for n in ("x1t_mm", "x1t_hi_set", "x1t_lo_set"))
        g_mm, g_hi_set, g_lo_set, x1_bv_set = (
            sem(n) for n in ("g_mm", "g_hi_set", "g_lo_set", "x1_bv_set"))
        vs_mm, vs_read, v_lo_set, w_set, wt_hi_set, wt_lo_set = (
            sem(n) for n in ("vs_mm", "vs_read", "v_lo_set", "w_set", "wt_hi_set", "wt_lo_set"))
        o_mm, den_set, den_inv_set, o_scale_set, y2_set = (
            sem(n) for n in ("o_mm", "den_set", "den_inv_set", "o_scale_set", "y2_set"))
        stats2_set, mean2_set, var2_set, rstd2_set, shift2_set, y_out_set = (
            sem(n) for n in ("stats2_set", "mean2_set", "var2_set", "rstd2_set", "shift2_set", "y_out_set"))

        by_chunk = "(c p) n -> p c n"
        block = ctx.enter_context(nc.Block())

        @block.sync
        def _(sp):
            def load_xt(q):
                if q.has(4):
                    sp.wait_ge(xt_lo_set, q.count(1, -3))
                sp.dma_start(xt_in[:, q.slot(4)], xt[q.index()]).then_inc(xt_loaded[q.slot(4)], 16)

            def load_x(q):
                if q.has(4):
                    sp.wait_ge(y1_set, q.count(1, -3))
                sp.dma_start(x_in[:, q.slot(4)], x[q.index()]).then_inc(x_loaded[q.slot(4)], 16)

            def load_adjt(q):
                if q.has(4):
                    sp.wait_ge(w_set, q.count(1, -3))
                sp.dma_start(adjt_in[:, q.slot(4)], adjt[q.index()]).then_inc(adjt_loaded[q.slot(4)], 16)

            def load(q):
                load_xt(q)
                load_x(q)
                load_adjt(q)

            def store(q):
                sp.wait_ge(y_out_set, q.count(1, 1))
                sp.dma_start(out[q.index()], y_out[:, q.slot(2)]).then_inc(stored[q.slot(2)], 16)

            sp.dma_start(wv0t_raw[:], Wv0t.rearrange(by_chunk, p=128)).then_inc(ld_wv0t, 16)
            load_xt(Pair(0, 0))
            sp.dma_start(ab_all[:], ab.partition_broadcast(128)).then_inc(ld_ab, 16)
            sp.dma_start(w_raw[:, :, D:2 * D], Wk0[1].rearrange(by_chunk, p=128)).then_inc(ld_w[1], 16)
            load_adjt(Pair(0, 0))
            sp.dma_start(wq1_raw[:], Wq1.rearrange(by_chunk, p=128)).then_inc(ld_m, 16)
            sp.dma_start(wk1_raw[:, :, 0:D], Wk1.rearrange(by_chunk, p=128)).then_inc(ld_m, 16)
            sp.dma_start(w_raw[:, :, 0:D], Wk0[0].rearrange(by_chunk, p=128)).then_inc(ld_w[0], 16)
            load_xt(Pair(0, 1))
            sp.wait_ge(bias_zero, 1)
            for r in (0, 32, 64):
                sp.dma_start(bias_raw[r:r + 3, :], bk0).then_inc(ld_bias, 16)
            sp.dma_start(v_raw[:, :, 0:D], Wv1t.rearrange(by_chunk, p=128)).then_inc(ld_v, 16)
            load_x(Pair(0, 0))
            load_adjt(Pair(0, 1))
            sp.dma_start(bv_all[:], bv1.partition_broadcast(128)).then_inc(ld_v, 16)
            load_x(Pair(0, 1))
            for n in range(2, AHEAD):
                load(Pair(0, n))
            with sp.Fori(0, PAIRS - 2 * UNROLL, UNROLL) as i:
                for k in range(UNROLL):
                    load(Pair(i, k + AHEAD))
                    store(Pair(i, k))
            for n in range(PAIRS - 2 * UNROLL, PAIRS):
                if n + AHEAD < PAIRS:
                    load(Pair(0, n + AHEAD))
                store(Pair(0, n))
            for n in range(2):
                sp.wait_ge(stored[n], 16 * (PAIRS // 2 + 1))

        @block.gpsimd
        def _(pool):
            nc.gpsimd.memset(bias_raw[:], 0.0).then_inc(bias_zero, 1)
            nc.gpsimd.memset(ident[:], 0.0).then_inc(ident_set, 1)
            nc.gpsimd.memset(ones_col[:], 1.0).then_inc(consts_set, 1)
            nc.gpsimd.memset(ones_bf[:], 1.0).then_inc(consts_set, 1)
            nc.gpsimd.memset(minus_half[:], -0.5).then_inc(consts_set, 1)
            pool.wait_ge(ident_set, 1)
            nc.gpsimd.affine_select(out=ident[:], in_=ident[:], compare_op=ALU.not_equal, fill=1.0, base=0,
                                    pattern=[[-1, 128]], channel_multiplier=1).then_inc(ident_set, 1)
            pool.wait_ge(consts_set, 3)

            def step(pair):
                q = pair[3]
                if q.exists():
                    if q.is_first():
                        pool.wait_ge(ld_v, 32)
                    pool.wait_ge(x1_set, q.count(1, 1))
                    for g in range(PG):
                        last = nc.gpsimd.tensor_tensor(x1_bv[:, q.slot(2), g], x1[:, g], bv_all[:], ALU.add)
                    last.then_inc(x1_bv_set, 1)
                q = pair[0]
                if q.exists():
                    pool.wait_ge(xt_hi_set, q.count(1, 1))
                    nc.gpsimd.tensor_tensor(xt_lo[:, q.slot(4)], xt_in[:, q.slot(4)],
                                            xt_hi[:, q.slot(4)].bitcast(F32),
                                            ALU.subtract).then_inc(xt_lo_set, 1)
                q = pair[1]
                if q.exists():
                    pool.wait_ge(adjt_loaded[q.slot(4)], q.turns(4, 1))
                    pool.wait_ge(e_max_set, q.count(1, 1))
                    nc.gpsimd.tensor_tensor(alpha[:], adjt_in[:, q.slot(4)], e_max[:],
                                            ALU.mult).then_inc(alpha_set, 1)
                q = pair[2]
                if q.exists():
                    pool.wait_ge(var1_set, q.count(1, 1))
                    nc.gpsimd.tensor_tensor(rstd1[:], var_eps1[:], minus_half[:],
                                            ALU.pow).then_inc(rstd1_set, 1)
                    pool.wait_ge(rstd1_set, q.count(1, 1))
                    nc.gpsimd.tensor_tensor(shift1[:], minus_mean1[:], rstd1[:],
                                            ALU.mult).then_inc(shift1_set, 1)
                q = pair[3]
                if q.exists():
                    pool.wait_ge(vs_read, q.count(2, 2))
                    nc.gpsimd.tensor_tensor(w_all[:], adjt_in[:, q.slot(4)], e_score[:],
                                            ALU.mult).then_inc(w_set, 1)
                q = pair[4]
                if q.exists():
                    pool.wait_ge(var2_set, q.count(1, 1))
                    nc.gpsimd.tensor_tensor(rstd2[:], var_eps2[:], minus_half[:],
                                            ALU.pow).then_inc(rstd2_set, 1)
                q = pair[3]
                if q.exists():
                    pool.wait_ge(wt_hi_set, q.count(1, 1))
                    nc.gpsimd.tensor_tensor(wt_lo[:], w_all[:], wt_hi[:].bitcast(F32),
                                            ALU.subtract).then_inc(wt_lo_set, 1)
                q = pair[4]
                if q.exists():
                    pool.wait_ge(rstd2_set, q.count(1, 1))
                    nc.gpsimd.tensor_tensor(shift2[:], minus_mean2[:], rstd2[:],
                                            ALU.mult).then_inc(shift2_set, 1)

            run_steps(pool, step)

        @block.scalar
        def _(act):
            act.dma_start(cols[:], columns).then_inc(ld_cols, 16)
            act.dma_start(w_raw[:, :, 2 * D:3 * D], Wk0[2].rearrange(by_chunk, p=128)).then_inc(ld_w[2], 16)

            def split_x(q):
                act.wait_ge(xt_loaded[q.slot(4)], q.turns(4, 1))
                nc.scalar.copy(xt_hi[:, q.slot(4)], xt_in[:, q.slot(4)]).then_inc(xt_hi_set, 1)

            split_x(Pair(0, 0))
            for n in (2, 1):
                act.wait_ge(ld_w[n], 16)
                of_n = slice(n * D, (n + 1) * D)
                nc.scalar.copy(w_hi[:, :, of_n], w_raw[:, :, of_n]).then_inc(w_hi_set, 1)
            act.wait_ge(s_cols_ready, 1)
            nc.scalar.copy(w_hi[:, :, 3 * D:], w_raw[:, :, 3 * D:]).then_inc(w_hi_set, 1)
            act.wait_ge(ld_w[0], 16)
            nc.scalar.copy(w_hi[:, :, 0:D], w_raw[:, :, 0:D]).then_inc(w_hi_set, 1)

            def high_m():
                act.wait_ge(m_setup_mm, 1)
                nc.scalar.copy(m_hi[:], m_setup[:, :, 0:D]).then_inc(m_hi_set, 1)

            def high_v_weights():
                act.wait_ge(m_cols_ready, 1)
                for g in range(PG):
                    nc.scalar.copy(gv_hi[:, g, :, 0:V_COLS], v_raw[:]).then_inc(m_hi_set, 1)

            def step(pair):
                q = pair[0]
                if q.exists():
                    if not q.is_first():
                        split_x(q)
                q = pair[3]
                if q.exists():
                    act.wait_ge(g_mm, q.count(1, 1))
                    for c in range(C):
                        last = nc.scalar.activation(gv_hi[:, :, c, V_COLS:], xg[:, c], ACT.Identity,
                                                    bias=u_col[:, c:c + 1])
                    last.then_inc(g_hi_set, 1)
                q = pair[1]
                if q.exists():
                    act.wait_ge(s_spread_mm, q.count(1, 1))
                    for g in range(PG):
                        nc.scalar.activation(e_full[:, g], spread_n[:, g], ACT.Exp, bias=s_cols[:, g, 0:1])
                        last = nc.scalar.activation(e_slope[:, g], spread_n[:, g], ACT.Exp,
                                                    bias=s_cols[:, g, 2:3], scale=SLOPE)
                    last.then_inc(e_set, 1)
                q = pair[2]
                if q.exists():
                    if q.is_first():
                        high_v_weights()
                q = pair[1]
                if q.exists():
                    if q.is_first():
                        high_m()
                q = pair[3]
                if q.exists():
                    act.wait_ge(vs_mm, q.count(2, 1))
                    nc.scalar.activation(e_score[:, 0], vo[:, 0, V_COLS:VS_COLS], ACT.Exp)
                    nc.scalar.activation(e_c[:, 0:1], vo[:, 0, D:D + 1], ACT.Exp, bias=c_const[:])
                    nc.scalar.copy(v_hi[:, 0, 0:D], vo[:, 0, 0:D]).then_inc(vs_read, 1)
                    act.wait_ge(vs_mm, q.count(2, 2))
                    nc.scalar.activation(e_score[:, 1], vo[:, 1, V_COLS:VS_COLS], ACT.Exp)
                    nc.scalar.activation(e_c[:, 1:2], vo[:, 1, D:D + 1], ACT.Exp, bias=c_const[:])
                    nc.scalar.copy(v_hi[:, 1, 0:D], vo[:, 1, 0:D]).then_inc(vs_read, 1)
                q = pair[2]
                if q.exists():
                    act.wait_ge(shift1_set, q.count(1, 1))
                    for g in range(PG):
                        last = nc.scalar.activation(x1[:, g], y1[:, g], ACT.Identity,
                                                    bias=shift1[:, g:g + 1], scale=rstd1[:, g:g + 1])
                    last.then_inc(x1_set, 1)
                q = pair[0]
                if q.exists():
                    act.wait_ge(z_mm, q.count(2, 1))
                    nc.scalar.copy(z_hi[:, q.slot(2), 0], z[:, 0, 0:D]).then_inc(z_hi_set, 1)
                q = pair[1]
                if q.exists():
                    act.wait_ge(t_set, q.count(1, 1))
                    nc.scalar.copy(t_hi[:], t_all[:]).then_inc(t_hi_set, 1)
                q = pair[3]
                if q.exists():
                    act.wait_ge(w_set, q.count(1, 1))
                    nc.scalar.copy(wt_hi[:], w_all[:]).then_inc(wt_hi_set, 1)
                q = pair[2]
                if q.exists():
                    act.wait_ge(x1t_mm, q.count(1, 1))
                    nc.scalar.copy(x1t_hi[:], xg[:]).then_inc(x1t_hi_set, 1)
                q = pair[0]
                if q.exists():
                    act.wait_ge(z_mm, q.count(2, 2))
                    nc.scalar.copy(z_hi[:, q.slot(2), 1], z[:, 1, 0:D]).then_inc(z_hi_set, 1)
                q = pair[4]
                if q.exists():
                    act.wait_ge(stored[q.slot(2)], q.turns(2, 1))
                    act.wait_ge(shift2_set, q.count(1, 1))
                    for g in range(PG):
                        last = nc.scalar.activation(y_out[:, q.slot(2), g], y2[:, g], ACT.Identity,
                                                    bias=shift2[:, g:g + 1], scale=rstd2[:, g:g + 1])
                    last.then_inc(y_out_set, 1)
                q = pair[1]
                if q.exists():
                    act.wait_ge(u_mm, q.count(1, 1))
                    nc.scalar.copy(u_hi[:], u[:]).then_inc(u_hi_set, 1)

            run_steps(act, step)

        @block.vector
        def _(dve):
            nc.vector.memset(w_raw[:, :, W_COLS - 1:W_COLS], 0.0).then_inc(stored[0], 16)
            nc.vector.memset(v_raw[:, :, V_COLS - 1:V_COLS], 0.0).then_inc(stored[1], 16)
            nc.vector.memset(v_hi[:, :, D:D + 1].bitcast(F32), 1.0)
            nc.vector.memset(v_hi[:, :, D + 1:D + 2].bitcast(F32), 0.0)
            nc.vector.memset(v_lo[:, :, D:D + 2].bitcast(F32), 0.0)
            nc.vector.memset(s_const[:, 3:4], 0.0)
            dve.wait_ge(ld_cols, 16)
            nc.vector.tensor_copy(wk1_raw[:, :, D:D + 1], cols[:, :, 4:5]).then_inc(bk_ready, 1)

            def low_w(lo, hi, nth):
                dve.wait_ge(w_hi_set, nth)
                nc.vector.tensor_tensor(w_lo[:, :, lo:hi], w_raw[:, :, lo:hi], w_hi[:, :, lo:hi].bitcast(F32),
                                        ALU.subtract).then_inc(w_lo_set, 1)

            low_w(2 * D, 3 * D, 1)
            low_w(D, 2 * D, 2)
            dve.wait_ge(s_setup_mm, 1)
            wji = s_setup[:, 0:2 * C].rearrange("p (c n) -> p c n", n=2)
            nc.vector.tensor_copy(w_raw[:, :, 3 * D:3 * D + 2], wji)
            nc.vector.tensor_scalar(w_raw[:, :, 3 * D + 2:3 * D + 3], wji[:, :, 0:1], SLOPE, None,
                                    ALU.mult).then_inc(s_cols_ready, 1)
            dve.wait_ge(ld_ab, 16)
            nc.vector.tensor_scalar(s_const[:, 0:1], s_setup[:, 8:9], ab_all[:], None, ALU.add)
            nc.vector.tensor_scalar(s_const[:, 2:3], s_setup[:, 8:9], ab_all[:], SLOPE, ALU.add, ALU.mult)
            nc.vector.tensor_copy(s_const[:, 1:2], s_setup[:, 9:10]).then_inc(s_const_set, 1)
            low_w(3 * D, W_COLS, 3)
            low_w(0, D, 4)
            dve.wait_ge(s_const_set, 1)

            def split_biases():
                dve.wait_ge(ld_bias, 48)
                nc.vector.tensor_copy(bias_hi[:], bias_raw[:]).then_inc(bias_split, 1)
                dve.wait_ge(bias_split, 1)
                nc.vector.tensor_tensor(bias_rest[:], bias_raw[:], bias_hi[:],
                                        ALU.subtract).then_inc(bias_split, 1)
                dve.wait_ge(bias_split, 2)
                nc.vector.tensor_copy(bias_mid[:], bias_rest[:]).then_inc(bias_split, 1)
                dve.wait_ge(bias_split, 3)
                nc.vector.tensor_tensor(bias_low[:], bias_rest[:], bias_mid[:],
                                        ALU.subtract).then_inc(bias_split, 1)
                dve.wait_ge(bias_split, 4)
                nc.vector.tensor_copy(bias_parts[0:32], bias_hi[0:32]).then_inc(bias_split, 1)
                nc.vector.tensor_copy(bias_parts[32:64], bias_mid[32:64]).then_inc(bias_split, 1)
                nc.vector.tensor_copy(bias_parts[64:128], bias_low[64:128]).then_inc(bias_split, 1)

            def place_attention_columns():
                dve.wait_ge(ld_v, 32)
                dve.wait_ge(m_setup_mm, 2)
                nc.vector.tensor_copy(u_col[:], u_setup[:, 0:C])
                nc.vector.tensor_copy(c_const[:], u_setup[:, C:C + 1])
                nc.vector.tensor_copy(v_raw[:, :, D:D + 1], m_setup[:, :, D:D + 1]).then_inc(m_cols_ready, 1)

            def low_m():
                dve.wait_ge(m_hi_set, 1)
                nc.vector.tensor_tensor(m_lo[:], m_setup[:, :, 0:D], m_hi[:].bitcast(F32),
                                        ALU.subtract).then_inc(m_lo_set, 1)

            def low_v_weights():
                dve.wait_ge(m_hi_set, 1 + PG)
                for g in range(PG):
                    nc.vector.tensor_tensor(gv_lo[:, g, :, 0:V_COLS], v_raw[:], gv_hi[:, g, :, 0:V_COLS].bitcast(F32),
                                            ALU.subtract).then_inc(m_lo_set, 1)

            def step(pair):
                q = pair[2]
                if q.exists():
                    dve.wait_ge(x1t_hi_set, q.count(1, 1))
                    nc.vector.tensor_tensor(x1t_lo[:], xg[:], x1t_hi[:].bitcast(F32),
                                            ALU.subtract).then_inc(x1t_lo_set, 1)
                q = pair[0]
                if q.exists():
                    dve.wait_ge(z_hi_set, q.count(2, 1))
                    nc.vector.tensor_tensor(s_cols[:, 0], z[:, 0, D:Z_COLS], s_const[:], ALU.add)
                    nc.vector.tensor_tensor(z_lo[:, q.slot(2), 0], z[:, 0, 0:D], z_hi[:, q.slot(2), 0].bitcast(F32),
                                            ALU.subtract).then_inc(z_lo_set, 1)
                    dve.wait_ge(z_hi_set, q.count(2, 2))
                    nc.vector.tensor_tensor(s_cols[:, 1], z[:, 1, D:Z_COLS], s_const[:], ALU.add)
                    nc.vector.tensor_tensor(z_lo[:, q.slot(2), 1], z[:, 1, 0:D], z_hi[:, q.slot(2), 1].bitcast(F32),
                                            ALU.subtract).then_inc(z_lo_set, 1)
                    if q.is_first():
                        split_biases()
                q = pair[3]
                if q.exists():
                    dve.wait_ge(o_mm, q.count(1, 1))
                    nc.vector.tensor_tensor(den[:], vo[:, :, D], e_c[:], ALU.mult).then_inc(den_set, 1)
                    dve.wait_ge(den_set, q.count(1, 1))
                    nc.vector.reciprocal(den_inv[:], den[:]).then_inc(den_inv_set, 1)
                q = pair[1]
                if q.exists():
                    dve.wait_ge(u_hi_set, q.count(1, 1))
                    nc.vector.tensor_tensor(u_lo[:], u[:], u_hi[:].bitcast(F32),
                                            ALU.subtract).then_inc(u_lo_set, 1)
                    if q.is_first():
                        place_attention_columns()
                q = pair[3]
                if q.exists():
                    dve.wait_ge(den_inv_set, q.count(1, 1))
                    nc.vector.tensor_tensor(o_scale[:], den_inv[:], e_c[:], ALU.mult).then_inc(o_scale_set, 1)
                    dve.wait_ge(x1_bv_set, q.count(1, 1))
                    wait(dve, y_out_set, q.count(1, 0))
                    dve.wait_ge(o_scale_set, q.count(1, 1))
                    for g in range(PG):
                        last = nc.vector.scalar_tensor_tensor(
                            out=y2[:, g], in0=vo[:, g, 0:D], scalar=o_scale[:, g:g + 1],
                            in1=x1_bv[:, q.slot(2), g], op0=ALU.mult, op1=ALU.add)
                    last.then_inc(y2_set, 1)
                q = pair[2]
                if q.exists():
                    dve.wait_ge(g_hi_set, q.count(1, 1))
                    for c in range(C):
                        last = nc.vector.scalar_tensor_tensor(
                            out=gv_lo[:, :, c, V_COLS:], in0=xg[:, c], scalar=u_col[:, c:c + 1],
                            in1=gv_hi[:, :, c, V_COLS:].bitcast(F32), op0=ALU.add, op1=ALU.subtract)
                    last.then_inc(g_lo_set, 1)
                q = pair[0]
                if q.exists():
                    dve.wait_ge(e_set, q.count(1, 1))
                    nc.vector.tensor_tensor(e_max[:], e_full[:], e_slope[:], ALU.max).then_inc(e_max_set, 1)
                q = pair[1]
                if q.exists():
                    dve.wait_ge(x_loaded[q.slot(4)], q.turns(4, 1))
                    dve.wait_ge(h_mm, q.count(1, 1))
                    nc.vector.scalar_tensor_tensor(out=y1[:], in0=h[:], scalar=0.0, in1=x_in[:, q.slot(4)],
                                                   op0=ALU.max, op1=ALU.add).then_inc(y1_set, 1)
                    dve.wait_ge(y1_set, q.count(1, 1))
                    for g in range(PG):
                        last = nc.vector.bn_stats(stats1[:, g], y1[:, g])
                    last.then_inc(stats1_set, 1)
                    dve.wait_ge(stats1_set, q.count(1, 1))
                q = pair[0]
                if q.exists():
                    dve.wait_ge(row_sum_mm, q.count(1, 1))
                    nc.vector.tensor_scalar(row_sum_eps[:], row_sum, ROW_EPS, None,
                                            ALU.add).then_inc(row_sum_set, 1)
                q = pair[1]
                if q.exists():
                    for g in range(PG):
                        last = nc.vector.bn_aggr(mean_var1[:, g], stats1[:, g])
                    last.then_inc(mean1_set, 1)
                q = pair[0]
                if q.exists():
                    dve.wait_ge(row_sum_set, q.count(1, 1))
                    nc.vector.reciprocal(row_inv[:], row_sum_eps[:]).then_inc(row_inv_set, 1)
                q = pair[1]
                if q.exists():
                    dve.wait_ge(mean1_set, q.count(1, 1))
                    nc.vector.tensor_scalar(minus_mean1[:], mean_var1[:, :, 0], -1.0, None, ALU.mult)
                    nc.vector.tensor_scalar(var_eps1[:], mean_var1[:, :, 1], LN_EPS, None,
                                            ALU.add).then_inc(var1_set, 1)
                    if q.is_first():
                        low_v_weights()
                q = pair[3]
                if q.exists():
                    dve.wait_ge(y2_set, q.count(1, 1))
                    for g in range(PG):
                        last = nc.vector.bn_stats(stats2[:, g], y2[:, g])
                    last.then_inc(stats2_set, 1)
                q = pair[0]
                if q.exists():
                    dve.wait_ge(inv_spread_mm, q.count(1, 1))
                    nc.vector.tensor_tensor(t_all[:], alpha[:], spread_n, ALU.mult).then_inc(t_set, 1)
                q = pair[3]
                if q.exists():
                    dve.wait_ge(stats2_set, q.count(1, 1))
                q = pair[2]
                if q.exists():
                    dve.wait_ge(vs_read, q.count(2, 1))
                    nc.vector.tensor_tensor(v_lo[:, 0, 0:D], vo[:, 0, 0:D], v_hi[:, 0, 0:D].bitcast(F32),
                                            ALU.subtract).then_inc(v_lo_set, 1)
                q = pair[3]
                if q.exists():
                    for g in range(PG):
                        last = nc.vector.bn_aggr(mean_var2[:, g], stats2[:, g])
                    last.then_inc(mean2_set, 1)
                    dve.wait_ge(mean2_set, q.count(1, 1))
                    nc.vector.tensor_scalar(minus_mean2[:], mean_var2[:, :, 0], -1.0, None, ALU.mult)
                    nc.vector.tensor_scalar(var_eps2[:], mean_var2[:, :, 1], LN_EPS, None,
                                            ALU.add).then_inc(var2_set, 1)
                q = pair[2]
                if q.exists():
                    dve.wait_ge(vs_read, q.count(2, 2))
                    nc.vector.tensor_tensor(v_lo[:, 1, 0:D], vo[:, 1, 0:D], v_hi[:, 1, 0:D].bitcast(F32),
                                            ALU.subtract).then_inc(v_lo_set, 1)
                q = pair[0]
                if q.exists():
                    dve.wait_ge(t_hi_set, q.count(1, 1))
                    nc.vector.tensor_tensor(t_lo[:], t_all[:], t_hi[:].bitcast(F32),
                                            ALU.subtract).then_inc(t_lo_set, 1)
                    if q.is_first():
                        low_m()

            run_steps(dve, step)

        @block.tensor
        def _(pe):
            mm = nc.tensor.matmul

            def split_product(to, stationary, moving, start, stop):
                terms = [(s[i], m[j]) for s, m in zip(stationary, moving) for i, j in ((0, 0), (0, 1), (1, 0))]
                for n, (s, m) in enumerate(terms):
                    last = mm(to, s, m, start=start and n == 0, stop=stop and n == len(terms) - 1,
                              skip_group_check=True)
                return last

            pe.wait_ge(ld_cols, 16)
            pe.wait_ge(ld_wv0t, 16)
            for c in range(C):
                for o in range(C):
                    last = mm(s_setup[:, 2 * c:2 * c + 2], wv0t_raw[:, o, c * 128:(c + 1) * 128], cols[:, o, 0:2],
                              start=(o == 0), stop=(o == C - 1))
            for o in range(C):
                last = mm(s_setup[:, 8:10], cols[:, o, 2:3].to_broadcast([128, 128]), cols[:, o, 0:2],
                          start=(o == 0), stop=(o == C - 1))
            last.then_inc(s_setup_mm, 1)

            def m_products():
                pe.wait_ge(ld_m, 32)
                pe.wait_ge(bk_ready, 1)
                for c in range(C):
                    for o in range(C):
                        last = mm(m_setup[:, c], wq1_raw[:, o, c * 128:(c + 1) * 128], wk1_raw[:, o, :],
                                  start=(o == 0), stop=(o == C - 1))
                last.then_inc(m_setup_mm, 1)

            def u_products():
                for c in range(C):
                    for o in range(C):
                        mm(u_setup[:, c:c + 1], wk1_raw[:, o, c * 128:(c + 1) * 128], cols[:, o, 3:4],
                           start=(o == 0), stop=(o == C - 1))
                for o in range(C):
                    last = mm(u_setup[:, C:C + 1], cols[:, o, 3:4].to_broadcast([128, 128]), cols[:, o, 4:5],
                              start=(o == 0), stop=(o == C - 1))
                last.then_inc(m_setup_mm, 1)

            def weights(lo, hi):
                return [(w_hi[:, c, lo:hi], w_lo[:, c, lo:hi]) for c in range(C)]

            def xt_of(q, g):
                return [(xt_hi[:, q.slot(4), c, g], xt_lo[:, q.slot(4), c, g]) for c in range(C)]

            def values_and_scores(g):
                split_product(vo[:, g, 0:VS_COLS], [(x1t_hi[:, c, g], x1t_lo[:, c, g]) for c in range(C)],
                              [(gv_hi[:, g, c], gv_lo[:, g, c]) for c in range(C)], True,
                                True).then_inc(vs_mm, 1)

            def step(pair):
                q = pair[1]
                if q.exists():
                    if q.is_first():
                        pe.wait_ge(ident_set, 2)
                        pe.wait_ge(consts_set, 3)
                    pe.wait_ge(z_lo_set, q.count(2, 2))
                    for g in range(PG):
                        last = nc.tensor.transpose(spread_n[:, g], s_cols[:, g, 1:2].to_broadcast([128, N]), ident[:])
                    last.then_inc(s_spread_mm, 1)
                q = pair[2]
                if q.exists():
                    if q.is_first():
                        pe.wait_ge(w_lo_set, 4)
                        pe.wait_ge(bias_split, 7)
                    wait(pe, y1_set, q.count(1, 0))
                    for g in range(PG):
                        mm(h[:, g], ones_bf[:], bias_parts[:], start=g == 0, stop=False, skip_group_check=True)
                        split_product(h[:, g], xt_of(q, g), weights(0, D), False, False)
                    pe.wait_ge(u_lo_set, q.count(1, 1))
                    for g in range(PG):
                        last = split_product(h[:, g], [(t_hi[:, g], t_lo[:, g])], [(u_hi[:, g], u_lo[:, g])],
                                             False, g == PG - 1)
                    last.then_inc(h_mm, 1)
                q = pair[3]
                if q.exists():
                    pe.wait_ge(g_lo_set, q.count(1, 1))
                    wait(pe, y2_set, q.count(1, 0))
                    values_and_scores(0)
                q = pair[1]
                if q.exists():
                    if q.is_first():
                        m_products()
                    pe.wait_ge(alpha_set, q.count(1, 1))
                    for g in range(PG):
                        last = mm(row_sum[:, g:g + 1], alpha[:, g], ones_col[:], start=True, stop=True)
                    last.then_inc(row_sum_mm, 1)
                q = pair[3]
                if q.exists():
                    values_and_scores(1)
                q = pair[0]
                if q.exists():
                    if q.is_first():
                        pe.wait_ge(w_lo_set, 3)
                    pe.wait_ge(xt_lo_set, q.count(1, 1))
                    split_product(z[:, 0, 0:Z_COLS], xt_of(q, 0), weights(2 * D, W_COLS), True,
                                  True).then_inc(z_mm, 1)
                q = pair[1]
                if q.exists():
                    pe.wait_ge(row_inv_set, q.count(1, 1))
                    for g in range(PG):
                        last = nc.tensor.transpose(spread_n[:, g], row_inv[:, g:g + 1].to_broadcast([128, N]),
                                                   ident[:])
                    last.then_inc(inv_spread_mm, 1)
                    if q.is_first():
                        pe.wait_ge(w_lo_set, 4)
                    for g in range(PG):
                        split_product(u[:, g], xt_of(q, g), weights(D, 2 * D), g == 0, False)
                q = pair[2]
                if q.exists():
                    if q.is_first():
                        pe.wait_ge(m_cols_ready, 1)
                    pe.wait_ge(x1_set, q.count(1, 1))
                    for g in range(PG):
                        for c in range(C):
                            last = nc.tensor.transpose(xg[:, c, g], x1[:, g, c * 128:(c + 1) * 128], ident[:])
                    last.then_inc(x1t_mm, 1)
                q = pair[0]
                if q.exists():
                    split_product(z[:, 1, 0:Z_COLS], xt_of(q, 1), weights(2 * D, W_COLS), True,
                                  True).then_inc(z_mm, 1)
                q = pair[1]
                if q.exists():
                    pe.wait_ge(t_lo_set, q.count(1, 1))
                    for g in range(PG):
                        last = split_product(u[:, g], [(t_hi[:, g], t_lo[:, g])],
                                             [(z_hi[:, q.slot(2), g], z_lo[:, q.slot(2), g])],
                                             False, g == PG - 1)
                    last.then_inc(u_mm, 1)
                    if q.is_first():
                        u_products()
                q = pair[3]
                if q.exists():
                    pe.wait_ge(wt_lo_set, q.count(1, 1))
                    pe.wait_ge(v_lo_set, q.count(2, 2))
                    for g in range(PG):
                        last = split_product(vo[:, g, 0:V_COLS], [(wt_hi[:, g], wt_lo[:, g])],
                                             [(v_hi[:, g], v_lo[:, g])], True, True)
                    last.then_inc(o_mm, 1)
                q = pair[2]
                if q.exists():
                    if q.is_first():
                        pe.wait_ge(m_lo_set, 1 + PG)
                    pe.wait_ge(x1t_lo_set, q.count(1, 1))
                    for c in range(C):
                        last = split_product(
                            xg[:, c], [(m_hi[:, k, c * 128:(c + 1) * 128], m_lo[:, k, c * 128:(c + 1) * 128])
                                       for k in range(C)],
                            [(x1t_hi[:, k], x1t_lo[:, k]) for k in range(C)], True, True)
                    last.then_inc(g_mm, 1)

            run_steps(pe, step)


def kernel(**inputs):
    import numpy as np
    import concourse.bacc as bacc
    from concourse.bass_utils import run_bass_kernel_spmd

    a = {k: np.asarray(v) for k, v in inputs.items()}
    x, adj = a["x"], a["adj"]
    aw = a["L0_gnn_aw"][:, 0]
    columns = np.stack([aw[:D], aw[D:], a["L0_gnn_bv"], a["L1_gnn_Wq_b"], a["L1_gnn_Wk_b"]], axis=-1)
    arrays = {
        "x": x.reshape(PAIRS, PG, N, D).transpose(0, 2, 1, 3),
        "xt": x.reshape(PAIRS, PG, N, C, 128).transpose(0, 4, 3, 1, 2),
        "adjt": adj.reshape(PAIRS, PG, N, N).transpose(0, 3, 1, 2),
        "columns": columns.reshape(C, 128, 5).transpose(1, 0, 2),
        "Wv0t": a["L0_gnn_Wv"].T,
        "ab": a["L0_gnn_ab"],
        "Wk0": a["L0_gnn_Wk"],
        "bk0": a["L0_gnn_bk"],
        "Wq1": a["L1_gnn_Wq_w"],
        "Wk1": a["L1_gnn_Wk_w"],
        "Wv1t": a["L1_gnn_Wv_w"].T,
        "bv1": a["L1_gnn_Wv_b"],
    }
    nc = bacc.Bacc("TRN2", target_bir_lowering=False, num_devices=1)
    feed, args = {}, []
    for name, value in arrays.items():
        value = np.ascontiguousarray(value)
        feed[f"in_{name}"] = value
        args.append(nc.dram_tensor(f"in_{name}", value.shape, F32, kind="ExternalInput").ap())
    args.append(nc.dram_tensor("out", (PAIRS, N, PG, D), F32, kind="ExternalOutput").ap())
    two_layer_graph_kernel(nc, *args)
    result = run_bass_kernel_spmd(nc, [feed], core_ids=[0]).results[0]["out"]
    return np.ascontiguousarray(result.transpose(0, 2, 1, 3).reshape(B, N, D))
```
